# Optimizing a Trainium2 kernel written in Bass

```python
import numpy as np
import jax
import jax.numpy as jnp

def _softmax(x, axis=-1):
    return jax.nn.softmax(x, axis=axis)

def _gelu(x):
    return jax.nn.gelu(x, approximate=True)

def _silu(x):
    return jax.nn.silu(x)

def _sigmoid(x):
    return jax.nn.sigmoid(x)

def _layernorm(x, axis=-1, eps=1e-05):
    m = jnp.mean(x, axis=axis, keepdims=True)
    v = jnp.var(x, axis=axis, keepdims=True)
    return (x - m) / jnp.sqrt(v + eps)

def _scatter_add(tgt, idx, src, axis=0):
    return tgt.at[idx].add(src)

def _segment_sum(src, seg, n):
    return jax.ops.segment_sum(src, seg, n)
kernel_name = 'mk_xattn_ffn_d2_seqx_r8_06e880'

def setup_inputs(seed: int=0):
    np.random.seed(seed)
    _w = jnp.asarray

    def _rec_inputs():
        import jax
        import jax.numpy as jnp
        _rk = jax.random.key(seed)
        x = 4.136e-05 + 0.9999 * jax.random.normal(jax.random.fold_in(_rk, 1), (4, 256, 256), jnp.float32)
        _lenS = 256 - jax.random.randint(jax.random.fold_in(_rk, 7), (4,), 0, max(1, 256 // 4) + 1, jnp.int32)
        _lenS2 = 256 - jax.random.randint(jax.random.fold_in(_rk, 8), (4,), 0, max(1, 256 // 4) + 1, jnp.int32)
        _ctx_1024P = jax.random.normal(jax.random.fold_in(_rk, 11), (4, 16, 128), jnp.float32)
        _ctx_1024c = jax.random.dirichlet(jax.random.fold_in(_rk, 511), 0.3 * jnp.ones((16,), jnp.float32), (4, 256))
        _ctx_1024t = jnp.einsum('bsk,bkd->bsd', _ctx_1024c, _ctx_1024P)
        _ctx_1024t = _ctx_1024t * jax.lax.rsqrt(jnp.mean(jnp.square(_ctx_1024t)) + 1e-12) * 0.953939
        ctx_1024 = -0.000292821 + 1.00034 * (_ctx_1024t + 0.3 * jax.random.normal(jax.random.fold_in(_rk, 611), (4, 256, 128), jnp.float32))
        return (x, ctx_1024)
    x, ctx_1024 = _rec_inputs()

    def _L0_xattn_setup():
        import jax, jax.numpy as jnp
        import numpy as np
        import math
        B, L, DM = (2, 256, 128)
        DS, DC, EXP = (16, 4, 2)
        DI = EXP * DM
        DR = math.ceil(DM / 16)
        DT_MIN, DT_MAX, DT_FLOOR = (0.001, 0.1, 0.0001)

        def _ssm_forward(hidden_states, z, in_proj_w, conv_w, conv_b, x_proj_w, dt_proj_w, dt_proj_b, A_log, D):
            b = hidden_states.shape[0]
            x = jnp.einsum('ed,bld->bel', in_proj_w, hidden_states)
            xp = jnp.pad(x, ((0, 0), (0, 0), (DC - 1, 0)))
            xc = jax.lax.conv_general_dilated(xp, conv_w[:, None, :], window_strides=(1,), padding='VALID', dimension_numbers=('NCH', 'OIH', 'NCH'), feature_group_count=DI)
            u = jax.nn.silu(xc + conv_b[None, :, None])
            x_dbl = jnp.einsum('ke,bel->bkl', x_proj_w, u)
            dt_lo = x_dbl[:, :DR]
            Bm = x_dbl[:, DR:DR + DS]
            Cm = x_dbl[:, DR + DS:]
            delta = jax.nn.softplus(jnp.einsum('er,brl->bel', dt_proj_w, dt_lo) + dt_proj_b[None, :, None])
            A = -jnp.exp(A_log)

            def step(state, xs):
                d_t, B_t, C_t, u_t = xs
                dA = jnp.exp(d_t[..., None] * A)
                state = state * dA + (d_t * u_t)[..., None] * B_t[:, None, :]
                y_t = jnp.einsum('ben,bn->be', state, C_t)
                return (state, y_t)
            xs = (jnp.moveaxis(delta, -1, 0), jnp.moveaxis(Bm, -1, 0), jnp.moveaxis(Cm, -1, 0), jnp.moveaxis(u, -1, 0))
            state0 = jnp.zeros((b, DI, DS), delta.dtype)
            _, ys = jax.lax.scan(step, state0, xs)
            y = jnp.moveaxis(ys, 0, -1)
            y = y + D[None, :, None] * u
            y = y * jax.nn.silu(z)
            return jnp.swapaxes(y, 1, 2)
        key = jax.random.key(seed)
        ks = jax.random.split(key, 8)
        hidden_states = jax.random.normal(ks[0], (B, L, DM), jnp.float32)
        z = jax.random.normal(ks[1], (B, DI, L), jnp.float32)
        in_proj_w = jax.random.normal(ks[2], (DI, DM), jnp.float32) * DM ** (-0.5)
        conv_w = jax.random.normal(ks[3], (DI, DC), jnp.float32) * DC ** (-0.5)
        conv_b = jnp.zeros((DI,), jnp.float32)
        x_proj_w = jax.random.normal(ks[4], (DR + 2 * DS, DI), jnp.float32) * DI ** (-0.5)
        dt_std = DR ** (-0.5)
        dt_proj_w = jax.random.uniform(ks[5], (DI, DR), jnp.float32, -dt_std, dt_std)
        dt = jnp.exp(jax.random.uniform(ks[6], (DI,), jnp.float32) * (math.log(DT_MAX) - math.log(DT_MIN)) + math.log(DT_MIN))
        dt = jnp.clip(dt, DT_FLOOR)
        dt_proj_b = dt + jnp.log(-jnp.expm1(-dt))
        A_log = jnp.log(jnp.broadcast_to(jnp.arange(1, DS + 1, dtype=jnp.float32), (DI, DS)))
        D = jnp.ones((DI,), jnp.float32)
        return dict(hidden_states=hidden_states, z=z, in_proj_w=in_proj_w, conv_w=conv_w, conv_b=conv_b, x_proj_w=x_proj_w, dt_proj_w=dt_proj_w, dt_proj_b=dt_proj_b, A_log=A_log, D=D)
    _L0_xattn_all = _L0_xattn_setup()
    _L0_xattn_in = {k: v for k, v in _L0_xattn_all.items() if k in ('in_proj_w', 'conv_w', 'conv_b', 'x_proj_w', 'dt_proj_w', 'dt_proj_b', 'A_log', 'D')}
    del _L0_xattn_all

    def _L0_ffn_setup():
        import jax, jax.numpy as jnp
        import numpy as np
        EPS_NORM = 1e-06
        EPS_SCALE = 1e-05

        def _rmsnorm(x, g):
            rms = jnp.sqrt(jnp.mean(x * x, axis=-1, keepdims=True) + EPS_NORM)
            return x / rms * g

        def _activation_quant(x):
            scale = 127.0 / jnp.clip(jnp.max(jnp.abs(x), axis=-1, keepdims=True), EPS_SCALE)
            return jnp.clip(jnp.round(x * scale), -128, 127) / scale

        def _weight_quant(w):
            scale = 1.0 / jnp.clip(jnp.mean(jnp.abs(w)), EPS_SCALE)
            return jnp.clip(jnp.round(w * scale), -1, 1) / scale

        def _bitlinear(x, w, g):
            x_norm = _rmsnorm(x, g)
            x_q = x_norm + jax.lax.stop_gradient(_activation_quant(x_norm) - x_norm)
            w_q = w + jax.lax.stop_gradient(_weight_quant(w) - w)
            return jnp.einsum('bsi,oi->bso', x_q, w_q)
        key = jax.random.key(seed)
        k_x, k_w1, k_w2 = jax.random.split(key, 3)
        d_model, d_ff = (256, 1024)
        B, S = (4, 256)
        x = jax.random.normal(k_x, (B, S, d_model), dtype=jnp.float32)
        w1 = jax.random.normal(k_w1, (d_ff, d_model), dtype=jnp.float32) * (1.0 / np.sqrt(d_model))
        w2 = jax.random.normal(k_w2, (d_model, d_ff), dtype=jnp.float32) * (1.0 / np.sqrt(d_ff))
        g1 = jnp.ones((d_model,), dtype=jnp.float32)
        g2 = jnp.ones((d_ff,), dtype=jnp.float32)
        return {'x': x, 'w1': w1, 'g1': g1, 'w2': w2, 'g2': g2}
    _L0_ffn_all = _L0_ffn_setup()
    _L0_ffn_in = {k: v for k, v in _L0_ffn_all.items() if k in ('w1', 'g1', 'w2', 'g2')}
    del _L0_ffn_all

    def _L1_xattn_setup():
        import jax, jax.numpy as jnp
        import numpy as np
        key = jax.random.key(seed)
        ks = jax.random.split(key, 6)
        B, L, N, C, D = (8, 64, 256, 128, 128)
        return {'teacher_logits': jax.random.normal(ks[0], (B, L, N), dtype=jnp.float32), 'teacher_features': jax.random.normal(ks[1], (B, N, C), dtype=jnp.float32), 'Wq': jax.random.normal(ks[2], (D, C), dtype=jnp.float32) * (1.0 / np.sqrt(C)), 'bq': jnp.zeros((D,), dtype=jnp.float32), 'Wk': jax.random.normal(ks[3], (D, C), dtype=jnp.float32) * (1.0 / np.sqrt(C)), 'bk': jnp.zeros((D,), dtype=jnp.float32)}
    _L1_xattn_all = _L1_xattn_setup()
    _L1_xattn_in = {k: v for k, v in _L1_xattn_all.items() if k in ('Wq', 'bq', 'Wk', 'bk')}
    del _L1_xattn_all

    def _L1_ffn_setup():
        import jax, jax.numpy as jnp
        import numpy as np
        E, K, H, I = (64, 8, 256, 96)
        key = jax.random.key(seed)
        k1, k2, k3, k4 = jax.random.split(key, 4)
        return {'hidden_states': jax.random.normal(k1, (1, 128, H), dtype=jnp.float32), 'w_gate': jax.random.normal(k2, (H, E), dtype=jnp.float32) * 0.02, 'w13': jax.random.normal(k3, (E, H, 2 * I), dtype=jnp.float32) * 0.02, 'w2': jax.random.normal(k4, (E, I, H), dtype=jnp.float32) * 0.02}
    _L1_ffn_all = _L1_ffn_setup()
    _L1_ffn_in = {k: v for k, v in _L1_ffn_all.items() if k in ('w_gate', 'w13', 'w2')}
    del _L1_ffn_all
    return {'x': x, 'ctx_1024': ctx_1024, 'L0_xattn_in_proj_w': _L0_xattn_in['in_proj_w'], 'L0_xattn_conv_w': _L0_xattn_in['conv_w'], 'L0_xattn_conv_b': _L0_xattn_in['conv_b'], 'L0_xattn_x_proj_w': _L0_xattn_in['x_proj_w'], 'L0_xattn_dt_proj_w': _L0_xattn_in['dt_proj_w'], 'L0_xattn_dt_proj_b': _L0_xattn_in['dt_proj_b'], 'L0_xattn_A_log': _L0_xattn_in['A_log'], 'L0_xattn_D': _L0_xattn_in['D'], 'L0_ffn_w1': _L0_ffn_in['w1'], 'L0_ffn_g1': _L0_ffn_in['g1'], 'L0_ffn_w2': _L0_ffn_in['w2'], 'L0_ffn_g2': _L0_ffn_in['g2'], 'L1_xattn_Wq': _L1_xattn_in['Wq'], 'L1_xattn_bq': _L1_xattn_in['bq'], 'L1_xattn_Wk': _L1_xattn_in['Wk'], 'L1_xattn_bk': _L1_xattn_in['bk'], 'L1_ffn_w_gate': _L1_ffn_in['w_gate'], 'L1_ffn_w13': _L1_ffn_in['w13'], 'L1_ffn_w2': _L1_ffn_in['w2']}

def reference(x, ctx_1024, L0_xattn_in_proj_w, L0_xattn_conv_w, L0_xattn_conv_b, L0_xattn_x_proj_w, L0_xattn_dt_proj_w, L0_xattn_dt_proj_b, L0_xattn_A_log, L0_xattn_D, L0_ffn_w1, L0_ffn_g1, L0_ffn_w2, L0_ffn_g2, L1_xattn_Wq, L1_xattn_bq, L1_xattn_Wk, L1_xattn_bk, L1_ffn_w_gate, L1_ffn_w13, L1_ffn_w2):
    import jax
    import jax.numpy as jnp

    def _L0_xattn_ref(hidden_states, z, in_proj_w, conv_w, conv_b, x_proj_w, dt_proj_w, dt_proj_b, A_log, D):
        import jax, jax.numpy as jnp
        import numpy as np
        import math
        B, L, DM = (2, 256, 128)
        DS, DC, EXP = (16, 4, 2)
        DI = EXP * DM
        DR = math.ceil(DM / 16)
        DT_MIN, DT_MAX, DT_FLOOR = (0.001, 0.1, 0.0001)

        def _ssm_forward(hidden_states, z, in_proj_w, conv_w, conv_b, x_proj_w, dt_proj_w, dt_proj_b, A_log, D):
            b = hidden_states.shape[0]
            x = jnp.einsum('ed,bld->bel', in_proj_w, hidden_states)
            xp = jnp.pad(x, ((0, 0), (0, 0), (DC - 1, 0)))
            xc = jax.lax.conv_general_dilated(xp, conv_w[:, None, :], window_strides=(1,), padding='VALID', dimension_numbers=('NCH', 'OIH', 'NCH'), feature_group_count=DI)
            u = jax.nn.silu(xc + conv_b[None, :, None])
            x_dbl = jnp.einsum('ke,bel->bkl', x_proj_w, u)
            dt_lo = x_dbl[:, :DR]
            Bm = x_dbl[:, DR:DR + DS]
            Cm = x_dbl[:, DR + DS:]
            delta = jax.nn.softplus(jnp.einsum('er,brl->bel', dt_proj_w, dt_lo) + dt_proj_b[None, :, None])
            A = -jnp.exp(A_log)

            def step(state, xs):
                d_t, B_t, C_t, u_t = xs
                dA = jnp.exp(d_t[..., None] * A)
                state = state * dA + (d_t * u_t)[..., None] * B_t[:, None, :]
                y_t = jnp.einsum('ben,bn->be', state, C_t)
                return (state, y_t)
            xs = (jnp.moveaxis(delta, -1, 0), jnp.moveaxis(Bm, -1, 0), jnp.moveaxis(Cm, -1, 0), jnp.moveaxis(u, -1, 0))
            state0 = jnp.zeros((b, DI, DS), delta.dtype)
            _, ys = jax.lax.scan(step, state0, xs)
            y = jnp.moveaxis(ys, 0, -1)
            y = y + D[None, :, None] * u
            y = y * jax.nn.silu(z)
            return jnp.swapaxes(y, 1, 2)
        return _ssm_forward(hidden_states, z, in_proj_w, conv_w, conv_b, x_proj_w, dt_proj_w, dt_proj_b, A_log, D)

    def _L0_ffn_ref(x, w1, g1, w2, g2):
        import jax, jax.numpy as jnp
        import numpy as np
        EPS_NORM = 1e-06
        EPS_SCALE = 1e-05

        def _rmsnorm(x, g):
            rms = jnp.sqrt(jnp.mean(x * x, axis=-1, keepdims=True) + EPS_NORM)
            return x / rms * g

        def _activation_quant(x):
            scale = 127.0 / jnp.clip(jnp.max(jnp.abs(x), axis=-1, keepdims=True), EPS_SCALE)
            return jnp.clip(jnp.round(x * scale), -128, 127) / scale

        def _weight_quant(w):
            scale = 1.0 / jnp.clip(jnp.mean(jnp.abs(w)), EPS_SCALE)
            return jnp.clip(jnp.round(w * scale), -1, 1) / scale

        def _bitlinear(x, w, g):
            x_norm = _rmsnorm(x, g)
            x_q = x_norm + jax.lax.stop_gradient(_activation_quant(x_norm) - x_norm)
            w_q = w + jax.lax.stop_gradient(_weight_quant(w) - w)
            return jnp.einsum('bsi,oi->bso', x_q, w_q)
        h = _bitlinear(x, w1, g1)
        h = jnp.square(jax.nn.relu(h))
        return _bitlinear(h, w2, g2)

    def _L1_xattn_ref(teacher_logits, teacher_features, Wq, bq, Wk, bk):
        import jax, jax.numpy as jnp
        import numpy as np
        query = jnp.einsum('bnc,dc->bnd', teacher_features, Wq) + bq
        key = jnp.einsum('bnc,dc->bnd', teacher_features, Wk) + bk
        energy = jnp.einsum('bnd,bmd->bnm', query, key)
        attention = jax.nn.softmax(energy, axis=-1)
        x_m = jnp.einsum('bln,bmn->blm', teacher_logits, attention)
        return x_m

    def _L1_ffn_ref(hidden_states, w_gate, w13, w2):
        import jax, jax.numpy as jnp
        import numpy as np
        E, K, H, I = (64, 8, 256, 96)
        orig_shape = hidden_states.shape
        x = hidden_states.reshape(-1, orig_shape[-1])
        T = x.shape[0]
        router_logits = x @ w_gate
        probs = jax.nn.softmax(router_logits, axis=-1)
        topk_w, topk_idx = jax.lax.top_k(probs, K)
        topk_w = topk_w / jnp.sum(topk_w, axis=-1, keepdims=True)
        combine = jnp.zeros((T, E), dtype=x.dtype).at[jnp.arange(T)[:, None], topk_idx].add(topk_w)
        h = jnp.einsum('th,ehd->etd', x, w13)
        gate, up = (h[..., :I], h[..., I:])
        act = jax.nn.silu(gate) * up
        y = jnp.einsum('eti,eih->eth', act, w2)
        out = jnp.einsum('eth,te->th', y, combine)
        return out.reshape(orig_shape)
    x = x + _L0_xattn_ref(ctx_1024, _layernorm(x, axis=-1), L0_xattn_in_proj_w, L0_xattn_conv_w, L0_xattn_conv_b, L0_xattn_x_proj_w, L0_xattn_dt_proj_w, L0_xattn_dt_proj_b, L0_xattn_A_log, L0_xattn_D)
    x = x + _L0_ffn_ref(_layernorm(x, axis=-1), L0_ffn_w1, L0_ffn_g1, L0_ffn_w2, L0_ffn_g2)
    x = x + _L1_xattn_ref(_layernorm(x, axis=-1), ctx_1024, L1_xattn_Wq, L1_xattn_bq, L1_xattn_Wk, L1_xattn_bk)
    x = x + _L1_ffn_ref(_layernorm(x, axis=-1), L1_ffn_w_gate, L1_ffn_w13, L1_ffn_w2)
    return x

_drawn_inputs = setup_inputs


def setup_inputs(seed=0):
    import zlib

    import numpy as np

    out = dict(_drawn_inputs(seed))
    spreads = {'L0_xattn_conv_b': (0.0, 0.1),
     'L0_xattn_D': (1.0, 0.2),
     'L0_ffn_g1': (1.0, 0.2),
     'L0_ffn_g2': (1.0, 0.2),
     'L1_xattn_bq': (0.0, 0.1),
     'L1_xattn_bk': (0.0, 0.8)}
    factors = {'L0_xattn_dt_proj_w': 5.16, 'L1_ffn_w_gate': 8.0, 'L1_ffn_w13': 8.0, 'L1_ffn_w2': 8.0}
    for name, (base, spread) in spreads.items():
        noise = np.random.default_rng([zlib.crc32(name.encode()), seed]).standard_normal(out[name].shape)
        drawn = base * np.exp(spread * noise) if base else spread * noise
        out[name] = jnp.asarray(drawn.astype(out[name].dtype))
    for name, factor in factors.items():
        out[name] = (out[name] * factor).astype(out[name].dtype)
    return out
```

```python
from contextlib import ExitStack

import concourse.bass as bass
from concourse import mybir

ALU = mybir.AluOpType
ACT = mybir.ActivationFunctionType
F32 = mybir.dt.float32
BF16 = mybir.dt.bfloat16
F16 = mybir.dt.float16
I32 = mybir.dt.int32
U32 = mybir.dt.uint32
AX = mybir.AxisListType.X

P = 128
ROUND = 12582912.0


class Steps:

    def __init__(self, engine, sem):
        self.engine, self.sem, self.n = engine, sem, 0

    def add(self, ins):
        self.n += 1
        ins.then_inc(self.sem, 1)

    def wait(self):
        self.engine.wait_ge(self.sem, self.n)

    def link(self, ins):
        self.add(ins)
        self.wait()


def mamba_ffn_attention_moe(nc, a, out, xln_dram, y_dram):
    B, L, DM = a["x"].shape
    DC = a["ctx_1024"].shape[2]
    DI = a["L0_xattn_in_proj_w"].shape[0]
    NH = DI // P
    DS = a["L0_xattn_A_log"].shape[1]
    TAPS = a["L0_xattn_conv_w"].shape[1]
    DR = a["L0_xattn_dt_proj_w"].shape[1]
    FF = a["L0_ffn_w1"].shape[0]
    E, H, I2 = a["L1_ffn_w13"].shape
    I = I2 // 2
    K = 8
    T = B * L
    NT = T // P
    LT = L // P
    KH = H // P
    FK = FF // P
    MT = T * K // P + E
    STEPS = NH * DS

    with ExitStack() as ctx:
        def sb(name, shape, dt=F32):
            return ctx.enter_context(nc.sbuf_tensor(name, shape, dt))

        def sem(name):
            return ctx.enter_context(nc.semaphore(name))

        EC = 4
        LATE = 12
        w13 = sb("w13", [P, E * KH * I2])
        w13e = w13[:, :].rearrange("p (e k d) -> p e k d", e=E, k=KH)
        late = w13[:, (E - LATE) * KH * I2:]
        big = sb("big", [P, 16384])
        area = sb("area", [P, 6400])
        xt = sb("xt", [P, NT, DM])
        ctxT = sb("ctxT", [P, T])
        attT = late[:, 0:2048].rearrange("p (k b m) -> p k b m", k=LT, b=B)
        w1qT = late[:, 2048:3072].bitcast(BF16)
        w2qT = late[:, 3072:4096].bitcast(BF16)
        ident = sb("ident", [P, P])
        identb = sb("identb", [P, P], BF16)
        g1 = sb("g1", [P, DM])
        g2 = sb("g2", [P, FF])
        wgate = sb("wgate", [P, KH, E])
        small = sb("small", [P, 620])
        ps = ctx.enter_context(nc.psum_tensor("ps", [P, 8, 512], F32))

        def bank(i, n=1):
            return ps[:, i:i + n, :].rearrange("p a c -> p (a c)")

        def part(t, at, n, dt=F32):
            v = t[:, at:at + n]
            return v if dt == F32 else v.bitcast(dt)

        u = part(big, 0, 2048).rearrange("p (h t) -> p h t", h=NH)
        delta = part(big, 2048, 2048).rearrange("p (h t) -> p h t", h=NH)
        du = part(big, 4096, 2048).rearrange("p (h t) -> p h t", h=NH)
        z = part(big, 6144, 2048).rearrange("p (h t) -> p h t", h=NH)
        lb = [part(big, 8192 + 1024 * i, 1024) for i in range(8)]
        ctx_raw = lb[0].rearrange("p (t c) -> p t c", t=NT)
        inw_raw = lb[1][:, 0:256].rearrange("p (h c) -> p h c", h=NH)
        wq_raw, wk_raw = lb[1][:, 256:384], lb[1][:, 384:512]
        xp_raw = lb[1][0:DR + 2 * DS, 512:768]
        dt_raw = lb[1][:, 768:784].rearrange("p (h r) -> p h r", h=NH)
        conv = [lb[2], lb[3]]
        w2e = big[0:I, :].rearrange("p (e d) -> p e d", e=E)
        w1_raw = part(area, 0, 2048)
        w2_raw = part(area, 2048, 2048)
        xin = part(area, 4096, NH * B * (L + TAPS - 1)).rearrange("p (h b l) -> p h b l", h=NH, b=B)
        w1q = part(area, 4096, 1024, BF16)
        w2q = part(area, 5120, 1024, BF16)
        cw = small[:, 0:8].rearrange("p (h k) -> p h k", h=NH)
        cb, dtb, dsk = small[:, 8:10], small[:, 10:12], small[:, 12:14]
        bq, bk = small[:, 14:15], small[:, 15:16]
        Aneg = small[:, 16:48].rearrange("p (h n) -> p h n", h=NH)
        mv = small[:, 48:64].rearrange("p (t s) -> p t s", t=NT)
        rstd, nbias = small[:, 64:72], small[:, 72:80]
        stat = small[:, 80:128].rearrange("p (t s) -> p t s", t=NT)
        sel = small[0:96, 128:144].bitcast(BF16)
        wsum, wmean, wscale = small[:, 144:146], small[:, 146:148], small[:, 148:150]
        nmax, asum, arec = small[:, 152:160], small[:, 160:168], small[:, 168:176]
        xpT = small[:, 176:384].rearrange("p (k c) -> p k c", k=NH)
        ones = small[:, 384:512]
        t8 = [small[:, 512 + 8 * i:520 + 8 * i] for i in range(13)]

        bcs = g2[0:96, 0:512].bitcast(BF16)
        dtT = sb("dtT", [DR, NH, P])
        ex = g2[:, 512:1024].rearrange("p (i l) -> p i l", i=2)
        wT = w2qT[:, 0:1024].bitcast(F32)
        qT = w1qT[:, :].bitcast(F32)
        kT = ctxT

        loaded = {n: sem("loaded_" + n) for n in ("ctx", "weights", "x", "ffn", "w13", "w2e")}
        names = ("consts ctxT_ps ctxT wT_ps wT xin_ps xin conv u_ready qk_ps qk xdbl_ps bc dt_lo dpre_ps xabs eneg lnp delta_ready "
                 "du_ready z_ready bmat cmat dA dbu scan hc ysum y_ready yT_ps x1 "
                 "energy att_max att_exp att_rec att_norm attT_ps attT wabs wtot wmean_ready wquant wqT_ps wqT "
                 "dve_chain act_chain pool_chain stats sq stored_out "
                 "ffn_var ffn_std rms_var rms_std ffn_norm xn q1 q1T_ps q1T h_ps h_relu h_sq h_ss hg r2_var r2_std q2 q2T_ps q2T o_ps x2 "
                 "at_var at_std at_norm at_ln at_lnT_ps at_lnT at_ps x3 ro_var ro_std ro_norm ro_ln ro_lnT_ps ro_lnT ro_consts "
                 "logits logit_shift logit_exp mask rank counts te te_ps te_row onehots onehots_read idx_ps idx xln_stored "
                 "m_T m_gT m_h m_silu m_act m_aT m_actT m_y_ps m_y out_tile").split()
        s = {n: sem(n) for n in names}
        gathered = [sem(f"gathered{r}") for r in range(4)]
        stored = [sem(f"stored{r}") for r in range(4)]
        picked = [sem(f"picked{t}") for t in range(NT)]

        r_buf = [part(big, 1024 * i, 1024) for i in range(2)]
        h_buf = [part(big, 2048 + 1024 * i, 1024) for i in range(2)]
        hg_buf = [part(big, 4096 + 1024 * i, 1024) for i in range(2)]
        q2_buf = [part(big, 6144 + 512 * i, 512, BF16) for i in range(2)]
        q2T_buf = [part(big, 7168 + 512 * i, 512, BF16).rearrange("p (k c) -> p k c", k=FK) for i in range(2)]
        xn = part(big, 8192, 2048).rearrange("p (t d) -> p t d", t=NT)
        q1 = part(big, 10240, 1024, BF16).rearrange("p (t d) -> p t d", t=NT)
        q1T = part(big, 11264, 1024, BF16).rearrange("p (k t) -> p k t", k=KH)
        w1T = w1qT.rearrange("p (k f) -> p k f", k=KH)
        w2T = w2qT.rearrange("p (k d) -> p k d", k=FK)
        ln = part(area, 0, 2048).rearrange("p (t d) -> p t d", t=NT)
        lnT = part(area, 2048, 2048).rearrange("p (t k c) -> p t k c", t=NT, k=KH)
        wdense = part(area, 5248, 512).rearrange("p (t e) -> p t e", t=NT)
        key = part(area, 5760, 512).rearrange("p (t e) -> p t e", t=NT)
        probs = g2[:, 0:512].rearrange("p (t e) -> p t e", t=NT)
        rest = g2[:, 512:1024].rearrange("p (t e) -> p t e", t=NT)
        mask = ctxT[:, 0:256].bitcast(BF16).rearrange("p (t e) -> p t e", t=NT)
        iota = ctxT[:, 256:320].bitcast(F16)
        RING = 4
        hot_r = [ctxT[:, 320 + 64 * i:384 + 64 * i].bitcast(F16) for i in range(RING)]
        hot_i = [ctxT[:, 576 + 64 * i:640 + 64 * i].bitcast(F16) for i in range(RING)]
        before = ctxT[:, 832:896].bitcast(BF16)
        onesb = ctxT[:, 896:960].bitcast(BF16)
        idx = g1[:, 0:128].bitcast(U32)
        slot = g1[:, 128:192].bitcast(U32)
        slot8 = g1[:, 192:256]
        ntile, tend, base = small[:, 176:240], small[:, 240:304], small[:, 304:368]
        te_row = wgate[0:1, :, :].rearrange("p k e -> p (k e)").bitcast(I32)
        icol, rcol = ctxT[:, 960:1024], stat.rearrange("p t s -> p (t s)")
        g_buf = [part(area, 2048 + 256 * i, 256) for i in range(4)]
        gT_buf = [part(area, 3072 + 256 * i, 256) for i in range(2)]
        silu_buf = [part(area, 3584 + 96 * i, 96) for i in range(2)]
        act_buf = [part(area, 3776 + 96 * i, 96) for i in range(2)]
        actT_buf = [part(area, 3968 + 128 * i, 128) for i in range(2)]
        y_buf = [part(area, 4224 + 256 * i, 256) for i in range(4)]
        picks = w13[:, 0:NT * K * DM].rearrange("p (s d) -> p s d", s=NT * K)

        def skewed(engine, parts):
            first, unroll = 5, 4
            loops = (MT - 3 - first) // unroll

            def body(j, static):
                for off, part_ in parts:
                    i = j + off
                    if 0 <= i < MT:
                        part_(i, i % 4, i // 4)

            for j in range(-2, first):
                body(j, True)
            with engine.Fori(0, loops) as q:
                for c in range(unroll):
                    for off, part_ in parts:
                        i0 = first + c + off
                        part_(q * unroll + i0, i0 % 4, q + i0 // 4)
            for j in range(first + loops * unroll, MT + 1):
                body(j, True)

        block = ctx.enter_context(nc.Block())

        @block.sync
        def _(sp):
            sp.dma_start(ctx_raw, a["ctx_1024"].rearrange("b (h p) d -> p (b h) d", p=P)).then_inc(loaded["ctx"], 16)
            loads = [
                (inw_raw, a["L0_xattn_in_proj_w"].rearrange("(h p) c -> p h c", p=P)),
                (wq_raw, a["L1_xattn_Wq"]), (wk_raw, a["L1_xattn_Wk"]),
                (xp_raw, a["L0_xattn_x_proj_w"]),
                (dt_raw, a["L0_xattn_dt_proj_w"].rearrange("(h p) r -> p h r", p=P)),
                (cw, a["L0_xattn_conv_w"].rearrange("(h p) k -> p h k", p=P)),
                *((cb[:, h:h + 1], a["L0_xattn_conv_b"][h * P:(h + 1) * P].rearrange("(p o) -> p o", o=1)) for h in range(NH)),
                *((dtb[:, h:h + 1], a["L0_xattn_dt_proj_b"][h * P:(h + 1) * P].rearrange("(p o) -> p o", o=1)) for h in range(NH)),
                *((dsk[:, h:h + 1], a["L0_xattn_D"][h * P:(h + 1) * P].rearrange("(p o) -> p o", o=1)) for h in range(NH)),
                (bq, a["L1_xattn_bq"].rearrange("(p o) -> p o", o=1)),
                (bk, a["L1_xattn_bk"].rearrange("(p o) -> p o", o=1)),
                (Aneg, a["L0_xattn_A_log"].rearrange("(h p) n -> p h n", p=P)),
            ]
            for dst, src in loads:
                sp.dma_start(dst, src).then_inc(loaded["weights"], 16)
            sp.dma_start(xt[:], a["x"].rearrange("b (h p) d -> p (b h) d", p=P)).then_inc(loaded["x"], 16)
            ffn_loads = [
                (w1_raw.rearrange("p (j c) -> p j c", j=FK), a["L0_ffn_w1"].rearrange("(j p) c -> p j c", p=P)),
                (w2_raw.rearrange("p (h f) -> p h f", h=NH), a["L0_ffn_w2"].rearrange("(h p) f -> p h f", p=P)),
                (g1[:], a["L0_ffn_g1"].partition_broadcast(P)),
                (wgate[:], a["L1_ffn_w_gate"].rearrange("(k p) e -> p k e", p=P)),
            ]
            for dst, src in ffn_loads:
                sp.dma_start(dst, src).then_inc(loaded["ffn"], 16)

            def load_w13(e):
                sp.dma_start(w13e[:, e:e + EC, :, :].rearrange("p e k d -> p (e k) d"), a["L1_ffn_w13"][e:e + EC].rearrange("e (k p) d -> p (e k) d", p=P)
                             ).then_inc(loaded["w13"], 16)

            for e in range(0, E - LATE, EC):
                load_w13(e)
            sp.wait_ge(s["x1"], NT // 2)
            sp.dma_start(g2[:], a["L0_ffn_g2"].partition_broadcast(P)).then_inc(loaded["ffn"], 16)
            sp.wait_ge(s["x2"], NT)
            for e in range(0, E, 16):
                sp.dma_start(w2e[:, e:e + 16, :], a["L1_ffn_w2"][e:e + 16].rearrange("e p d -> p e d")).then_inc(loaded["w2e"], 16)
            sp.wait_ge(s["x3"], NT)
            for e in range(E - LATE, E, EC):
                load_w13(e)
            sp.wait_ge(s["ro_ln"], NT)
            sp.dma_start(xln_dram.rearrange("(t p) d -> p t d", p=P), ln).then_inc(s["xln_stored"], 16)

            def store(i, r, n4):
                sp.wait_ge(s["m_y"], i + 1)
                sp.dma_start(y_dram[bass.ds(i * P, P), :], y_buf[r]).then_inc(stored[r], 16)

            skewed(sp, [(-1, store)])
            for t in range(NT):
                sp.wait_ge(s["out_tile"], t + 1)
                sp.dma_start(out.rearrange("b (h p) d -> p (b h) d", p=P)[:, t, :], xt[:, t, :]).then_inc(s["stored_out"], 16)
            sp.wait_ge(s["stored_out"], 16 * NT)

        @block.gpsimd
        def _(pool):
            st = Steps(pool, s["pool_chain"])
            st.add(pool.memset(ident[:], 0.0))
            st.add(pool.memset(identb[:], 0.0))
            st.add(pool.memset(sel, 0.0))
            st.add(pool.memset(ones, 1.0))
            st.add(pool.memset(xin[:, :, :, 0:TAPS - 1], 0.0))
            st.wait()
            st.link(pool.affine_select(out=ident[:], in_=ident[:], compare_op=ALU.not_equal, fill=1.0, base=0, pattern=[[-1, P]], channel_multiplier=1))
            st.link(pool.affine_select(out=identb[:], in_=identb[:], compare_op=ALU.not_equal, fill=1.0, base=0, pattern=[[-1, P]], channel_multiplier=1))
            for g in range(3):
                st.link(pool.affine_select(out=sel, in_=sel, compare_op=ALU.not_equal, fill=1.0, base=-32 * g, pattern=[[-1, 32]], channel_multiplier=1))
            pool.sem_inc(s["consts"], 1)

            for t in range(NT):
                pool.wait_ge(s["att_rec"], t + 1)
                pool.tensor_scalar(ex[:, t % 2, :], ex[:, t % 2, :], arec[:, t:t + 1], None, ALU.mult).then_inc(s["att_norm"], 1)
            pool.wait_ge(s["wmean_ready"], 1)
            pool.wait_ge(s["conv"], 2)
            for i, (raw, q) in enumerate(((w1_raw, w1q), (w2_raw, w2q))):
                st.link(pool.tensor_scalar(raw, raw, wscale[:, i:i + 1], ROUND, ALU.mult, ALU.add))
                st.link(pool.tensor_scalar(raw, raw, ROUND + 1.0, ROUND - 1.0, ALU.min, ALU.max))
                pool.tensor_scalar(q, raw, -ROUND, 1.0, ALU.add, ALU.mult).then_inc(s["wquant"], 1)
            st.add(pool.iota(iota, [[1, P]], base=0, channel_multiplier=0, allow_small_or_imprecise_dtypes=True))
            st.add(pool.iota(t8[0], [[P, NT]], base=0, channel_multiplier=1, allow_small_or_imprecise_dtypes=True))
            st.link(pool.memset(onesb, 1.0))
            pool.affine_select(out=before, in_=onesb, compare_op=ALU.is_gt, fill=0.0, base=0, pattern=[[1, P]], channel_multiplier=-1).then_inc(s["ro_consts"], 1)
            pool.wait_ge(loaded["ffn"], 16 * 5)
            for t in range(NT):
                pool.wait_ge(s["h_sq"], t + 1)
                if t >= 2:
                    pool.wait_ge(s["q2"], t - 1)
                pool.tensor_tensor(hg_buf[t % 2], h_buf[t % 2], g2[:], ALU.mult).then_inc(s["hg"], 1)
            pool.wait_ge(s["idx"], 1)
            pool.wait_ge(s["xln_stored"], 16)
            for i in range(MT):
                if i >= 4:
                    pool.wait_ge(s["m_T"], i - 3)
                pool.indirect_dma_start(g_buf[i % 4], None, xln_dram, bass.IndirectOffsetOnAxis(ap=idx[:, i:i + 1], axis=0)).then_inc(gathered[i % 4], 16)
            for r in range(4):
                pool.wait_ge(stored[r], 16 * (MT // 4))
            for n in range(NT * K):
                pool.indirect_dma_start(picks[:, n, :], None, y_dram, bass.IndirectOffsetOnAxis(ap=slot[:, n:n + 1], axis=0)).then_inc(picked[n // K], 16)

        @block.vector
        def _(v):
            st = Steps(v, s["dve_chain"])
            v.wait_ge(loaded["x"], 16)
            for t in range(NT):
                st.link(v.bn_stats(stat[:, t, :], xt[:, t, :]))
                st.link(v.bn_aggr(mv[:, t, :], stat[:, t, :]))
            v.tensor_scalar(rstd, mv[:, :, 1], 1e-5, None, ALU.add).then_inc(s["stats"], 1)
            v.wait_ge(s["wT_ps"], 1)
            v.tensor_copy(wT, bank(2)).then_inc(s["wT"], 1)
            v.wait_ge(s["wT_ps"], 2)
            raw = ps[:, 3, 0:128].rearrange("p (k c) -> p k c", k=NH)
            for g in range(3):
                st.add(v.tensor_copy(xpT[:, :, 32 * g:32 * g + 32], raw[:, :, DR:DR + 32]))
            st.add(v.tensor_copy(xpT[:, :, 96:96 + DR], raw[:, :, 0:DR]))
            v.tensor_copy(dtT[:, :, :], ps[0:DR, 3, 128:384].rearrange("p (h c) -> p h c", h=NH)).then_inc(s["wT"], 1)
            st.wait()
            v.wait_ge(s["sq"], 1)
            st.link(v.reciprocal(rstd, rstd))
            v.scalar_tensor_tensor(out=nbias, in0=mv[:, :, 0], scalar=-1.0, in1=rstd, op0=ALU.mult, op1=ALU.mult).then_inc(s["stats"], 1)
            for h in range(NH):
                v.wait_ge(s["xin"], h + 1)
                c = conv[h].rearrange("p (b l) -> p b l", b=B)
                st.link(v.tensor_scalar(c, xin[:, h, :, TAPS - 1:TAPS - 1 + L], cw[:, h, TAPS - 1:TAPS], cb[:, h:h + 1], ALU.mult, ALU.add))
                for k in range(TAPS - 1):
                    ins = v.scalar_tensor_tensor(out=c, in0=xin[:, h, :, k:k + L], scalar=cw[:, h, k:k + 1], in1=c, op0=ALU.mult, op1=ALU.add)
                    if k < TAPS - 2:
                        st.link(ins)
                    else:
                        ins.then_inc(s["conv"], 1)
            v.wait_ge(s["xdbl_ps"], 1)
            v.tensor_copy(lb[7][0:DR, :], ps[0:DR, 2:4, :].rearrange("p a c -> p (a c)")).then_inc(s["dt_lo"], 1)
            bc = ps[0:96, 0:2, :].rearrange("p a c -> p (a c)")
            hi = lb[4][0:96, 0:512].bitcast(BF16)
            mid = lb[4][0:96, 512:1024].bitcast(BF16)
            r1, r2 = lb[5][0:96, :], lb[6][0:96, :]
            st.link(v.tensor_copy(hi, bc))
            st.add(v.tensor_copy(bcs[0:32, :], hi[0:32, :]))
            st.link(v.tensor_tensor(r1, bc, hi, ALU.subtract))
            st.link(v.tensor_copy(mid, r1))
            st.add(v.tensor_copy(bcs[32:64, :], mid[32:64, :]))
            st.link(v.tensor_tensor(r2, r1, mid, ALU.subtract))
            v.tensor_copy(bcs[64:96, :], r2[64:96, :]).then_inc(s["bc"], 1)
            v.wait_ge(s["bc"], 1)
            for h in range(NH):
                e, w = (lb[1], lb[2]) if h == 0 else (lb[5], lb[6])
                v.wait_ge(s["xabs"], h + 1)
                pre = bank(4 + 2 * h, 2)
                st.add(v.tensor_scalar(du[:, h, :], pre, dtb[:, h:h + 1], 0.0, ALU.add, ALU.max))
                v.wait_ge(s["eneg"], h + 1)
                st.link(v.tensor_scalar(w, e, 1.0, None, ALU.add))
                st.link(v.scalar_tensor_tensor(out=w, in0=w, scalar=-1.0, in1=e, op0=ALU.add, op1=ALU.subtract))
                st.link(v.tensor_tensor(w, du[:, h, :], w, ALU.subtract))
                v.wait_ge(s["lnp"], h + 1)
                v.tensor_tensor(delta[:, h, :], delta[:, h, :], w, ALU.add).then_inc(s["delta_ready"], 1)
                v.wait_ge(s["delta_ready"], h + 1)
                v.tensor_tensor(du[:, h, :], delta[:, h, :], u[:, h, :], ALU.mult).then_inc(s["du_ready"], 1)
            v.wait_ge(s["du_ready"], 2)
            for i in range(2):
                st.add(v.memset(lb[i].rearrange("p (b l) -> p b l", b=B)[:, :, 0:1], 0.0))
            st.wait()

            for n in range(STEPS):
                h, i = n // DS, n % 2
                v.wait_ge(s["bmat"], n + 1)
                v.tensor_tensor(lb[2 + i], bank(0, 2), du[:, h, :], ALU.mult).then_inc(s["dbu"], 1)
                v.wait_ge(s["dbu"], n + 1)
                v.wait_ge(s["dA"], n + 1)
                v.tensor_tensor_scan(lb[4 + i], lb[i], lb[2 + i], 0.0, ALU.mult, ALU.add).then_inc(s["scan"], 1)
                if n < NT:
                    v.wait_ge(s["energy"], n + 1)
                    v.tensor_reduce(nmax[:, n:n + 1], ps[:, 6, 0:L], AX, ALU.max, negate=True).then_inc(s["att_max"], 1)
                if 1 <= n <= NT:
                    v.wait_ge(s["att_exp"], n)
                    v.reciprocal(arec[:, n - 1:n], asum[:, n - 1:n]).then_inc(s["att_rec"], 1)
                if n == NT + 2:
                    v.wait_ge(s["wtot"], 1)
                    st.link(v.tensor_scalar(wmean, ps[:, 6, 0:2], 1.0 / (FF * DM), 1e-5, ALU.mult, ALU.max))
                    v.reciprocal(wscale, wmean).then_inc(s["wmean_ready"], 1)
                v.wait_ge(s["scan"], n + 1)
                v.wait_ge(s["cmat"], n + 1)
                if n >= 2:
                    v.wait_ge(s["ysum"], n - 1)
                v.tensor_tensor(lb[6 + i], bank(2, 2), lb[4 + i], ALU.mult).then_inc(s["hc"], 1)
                if n % DS == DS - 1:
                    v.wait_ge(s["ysum"], n + 1)
                    st.link(v.scalar_tensor_tensor(out=u[:, h, :], in0=u[:, h, :], scalar=dsk[:, h:h + 1], in1=bank(4, 2), op0=ALU.mult, op1=ALU.add))
                    v.wait_ge(s["z_ready"], NT)
                    v.tensor_tensor(du[:, h, :], u[:, h, :], z[:, h, :], ALU.mult).then_inc(s["y_ready"], 1)
            for q in range(NT // 2):
                v.wait_ge(s["yT_ps"], q + 1)
                v.tensor_tensor(xt[:, 2 * q:2 * q + 2, :].rearrange("p t c -> p (t c)"), bank(q),
                                xt[:, 2 * q:2 * q + 2, :].rearrange("p t c -> p (t c)"), ALU.add).then_inc(s["x1"], 1)

            def statistics(ready, var, std, norm):
                for t in range(NT):
                    v.wait_ge(*ready(t))
                    st.link(v.bn_stats(stat[:, t, :], xt[:, t, :]))
                    st.link(v.bn_aggr(mv[:, t, :], stat[:, t, :]))
                v.tensor_scalar(rstd, mv[:, :, 1], 1e-5, None, ALU.add).then_inc(s[var], 1)
                v.wait_ge(s[std], 1)
                st.link(v.reciprocal(rstd, rstd))
                if norm:
                    v.scalar_tensor_tensor(out=nbias, in0=mv[:, :, 0], scalar=-1.0, in1=rstd, op0=ALU.mult, op1=ALU.mult).then_inc(s[norm], 1)

            statistics(lambda t: (s["x1"], t // 2 + 1), "ffn_var", "ffn_std", None)
            st.link(v.tensor_tensor(t8[1], rstd, rstd, ALU.mult))
            st.link(v.tensor_tensor(t8[1], t8[1], mv[:, :, 1], ALU.mult))
            v.tensor_scalar(t8[1], t8[1], 1e-6, None, ALU.add).then_inc(s["rms_var"], 1)
            v.wait_ge(s["rms_std"], 1)
            st.link(v.reciprocal(t8[1], t8[1]))
            st.link(v.tensor_tensor(rstd, rstd, t8[1], ALU.mult))
            v.scalar_tensor_tensor(out=nbias, in0=mv[:, :, 0], scalar=-1.0, in1=rstd, op0=ALU.mult, op1=ALU.mult).then_inc(s["ffn_norm"], 1)
            for t in range(NT):
                v.wait_ge(s["xn"], t + 1)
                st.link(v.tensor_tensor(xn[:, t, :], xn[:, t, :], g1[:], ALU.mult))
                st.link(v.tensor_reduce(t8[2][:, t:t + 1], xn[:, t, :], AX, ALU.max, apply_absolute_value=True))
            st.link(v.tensor_scalar(t8[2], t8[2], 1e-5, None, ALU.max))
            st.link(v.reciprocal(t8[3], t8[2]))
            st.link(v.tensor_scalar(t8[3], t8[3], 127.0, None, ALU.mult))
            st.link(v.tensor_scalar(t8[4], t8[2], 1.0 / 127.0, wmean[:, 0:1], ALU.mult, ALU.mult))
            for t in range(NT):
                st.link(v.tensor_scalar(xn[:, t, :], xn[:, t, :], t8[3][:, t:t + 1], ROUND, ALU.mult, ALU.add))
                v.tensor_scalar(q1[:, t, :], xn[:, t, :], -ROUND, 127.0, ALU.add, ALU.min).then_inc(s["q1"], 1)
            for g in range(2):
                v.wait_ge(s["q1T_ps"], g + 1)
                v.tensor_scalar(q1T[:, :, 512 * g:512 * g + 512].rearrange("p k (t c) -> p t k c", t=4),
                                bank(6 + g).bitcast(BF16).rearrange("p (t k c) -> p t k c", t=4, k=KH), -128.0, None, ALU.max).then_inc(s["q1T"], 1)

            def ffn_max(t):
                v.wait_ge(s["h_ss"], t + 1)
                v.tensor_scalar(t8[5][:, t:t + 1], t8[5][:, t:t + 1], 1.0 / FF, 1e-6, ALU.mult, ALU.add).then_inc(s["r2_var"], 1)
                v.wait_ge(s["hg"], t + 1)
                st.link(v.tensor_reduce(t8[6][:, t:t + 1], hg_buf[t % 2], AX, ALU.max, apply_absolute_value=True))

            def ffn_quant(t):
                c = slice(t, t + 1)
                v.wait_ge(s["r2_std"], t + 1)
                st.link(v.reciprocal(t8[5][:, c], t8[5][:, c]))
                st.link(v.tensor_scalar(t8[6][:, c], t8[6][:, c], t8[5][:, c], 1e-5, ALU.mult, ALU.max))
                st.link(v.reciprocal(t8[7][:, c], t8[6][:, c]))
                st.link(v.tensor_scalar(t8[7][:, c], t8[7][:, c], 127.0, None, ALU.mult))
                st.add(v.tensor_scalar(t8[8][:, c], t8[6][:, c], 1.0 / 127.0, wmean[:, 1:2], ALU.mult, ALU.mult))
                st.link(v.tensor_scalar(hg_buf[t % 2], hg_buf[t % 2], t8[5][:, c], t8[7][:, c], ALU.mult, ALU.mult))
                if t >= 2:
                    v.wait_ge(s["q2T_ps"], t - 1)
                v.tensor_scalar(q2_buf[t % 2], hg_buf[t % 2], ROUND, -ROUND, ALU.add, ALU.add).then_inc(s["q2"], 1)

            def ffn_turn(t):
                v.wait_ge(s["q2T_ps"], t + 1)
                if t >= 2:
                    v.wait_ge(s["o_ps"], t - 1)
                v.tensor_scalar(q2T_buf[t % 2].rearrange("p k c -> p (k c)"), bank(4 + t % 2).bitcast(BF16), -128.0, 127.0, ALU.max, ALU.min).then_inc(s["q2T"], 1)

            def ffn_add(t):
                v.wait_ge(s["o_ps"], t + 1)
                v.scalar_tensor_tensor(out=xt[:, t, :], in0=ps[:, 6 + t % 2, 0:DM], scalar=t8[8][:, t:t + 1], in1=xt[:, t, :], op0=ALU.mult, op1=ALU.add).then_inc(s["x2"], 1)

            for j in range(NT + 3):
                for off, part_ in ((0, ffn_max), (-1, ffn_quant), (-2, ffn_turn), (-3, ffn_add)):
                    if 0 <= j + off < NT:
                        part_(j + off)

            statistics(lambda t: (s["x2"], t + 1), "at_var", "at_std", "at_norm")
            for t in range(NT):
                v.wait_ge(s["at_ps"], t + 1)
                v.tensor_tensor(xt[:, t, :], ps[:, 4 + t % 4, 0:L], xt[:, t, :], ALU.add).then_inc(s["x3"], 1)

            statistics(lambda t: (s["x3"], t + 1), "ro_var", "ro_std", "ro_norm")
            v.wait_ge(s["logits"], 1)
            logits = bank(4).rearrange("p (t e) -> p t e", t=NT)
            st.link(v.tensor_reduce(t8[1], logits, AX, ALU.max))
            v.tensor_tensor(probs, logits, t8[1].unsqueeze(2).broadcast_to([P, NT, E]), ALU.subtract).then_inc(s["logit_shift"], 1)
            v.wait_ge(s["logit_exp"], 1)
            st.link(v.tensor_reduce(t8[2], probs, AX, ALU.add))
            st.link(v.reciprocal(t8[2], t8[2]))
            st.link(v.tensor_tensor(probs, probs, t8[2].unsqueeze(2).broadcast_to([P, NT, E]), ALU.mult))
            for t in range(NT):
                st.link(v.max(out=slot8[:, K * t:K * t + K], in_=probs[:, t, :]))
                st.link(v.match_replace(rest[:, t, :], slot8[:, K * t:K * t + K], probs[:, t, :], -1.0))
            v.tensor_scalar(mask, rest, 0.0, None, ALU.is_lt).then_inc(s["mask"], 1)
            st.link(v.tensor_reduce(t8[3], slot8.rearrange("p (t k) -> p t k", t=NT), AX, ALU.add))
            st.link(v.reciprocal(t8[3], t8[3]))
            v.wait_ge(s["mask"], 1)
            st.link(v.tensor_tensor(wdense, probs, mask, ALU.mult))
            st.link(v.tensor_tensor(wdense, wdense, t8[3].unsqueeze(2).broadcast_to([P, NT, E]), ALU.mult))
            v.wait_ge(s["counts"], 1)
            st.link(v.tensor_scalar(ntile, ps[:, 6, 0:E], 1.0 / P, 0.5 - 0.5 / P, ALU.mult, ALU.add))
            st.link(v.tensor_scalar(ntile, ntile, ROUND, -ROUND, ALU.add, ALU.add))
            st.link(v.tensor_tensor_scan(tend, ones[:, 0:E], ntile, 0.0, ALU.mult, ALU.add))
            st.link(v.tensor_scalar(rest[:, 0, :], tend, t8[0][:, 0:1], None, ALU.is_le))
            st.link(v.tensor_reduce(t8[4][:, 0:1], rest[:, 0, :], AX, ALU.add))
            v.tensor_scalar(t8[4][:, 0:1], t8[4][:, 0:1], float(E - 1), None, ALU.min).then_inc(s["te"], 1)
            st.link(v.tensor_tensor(base, tend, ntile, ALU.subtract))
            st.link(v.tensor_scalar(base, base, float(P), 1.0, ALU.mult, ALU.add))
            v.wait_ge(s["rank"], 1)
            st.link(v.tensor_tensor(key, bank(5).rearrange("p (t e) -> p t e", t=NT), base.unsqueeze(1).broadcast_to([P, NT, E]), ALU.add))
            st.link(v.tensor_tensor(key, key, mask, ALU.mult))
            for t in range(NT):
                st.add(v.max(out=slot8[:, K * t:K * t + K], in_=key[:, t, :]))
            st.wait()
            s0 = rest[:, 1, :]
            st.link(v.tensor_scalar(s0, slot8, -1.0, None, ALU.add))
            st.add(v.tensor_copy(slot, s0))
            st.link(v.tensor_scalar(icol, s0, 1.0 / P, -(0.5 - 0.5 / P), ALU.mult, ALU.add))
            st.link(v.tensor_scalar(icol, icol, ROUND, -ROUND, ALU.add, ALU.add))
            rc = rest[:, 2, :]
            st.link(v.scalar_tensor_tensor(out=rc, in0=icol, scalar=-float(P), in1=s0, op0=ALU.mult, op1=ALU.add))
            v.wait_ge(s["te_ps"], 1)
            v.tensor_copy(te_row, ps[0:1, 7, 0:P]).then_inc(s["te_row"], 1)
            v.wait_ge(s["ro_consts"], 1)
            for n in range(NT * K):
                if n >= RING:
                    v.wait_ge(s["onehots_read"], n - RING + 1)
                st.add(v.tensor_scalar(hot_r[n % RING], iota, rc[:, n:n + 1], None, ALU.is_equal))
                v.tensor_scalar(hot_i[n % RING], iota, icol[:, n:n + 1], t8[0][:, n // K:n // K + 1], ALU.is_equal, ALU.mult).then_inc(s["onehots"], 1)
            v.wait_ge(s["idx_ps"], 1)
            v.tensor_copy(idx, ps[:, 6, 0:P]).then_inc(s["idx"], 1)

            def gate_up(i, r, n4):
                v.wait_ge(s["m_silu"], i + 1)
                if not isinstance(i, int) or i >= 2:
                    v.wait_ge(s["m_aT"], i - 1)
                v.tensor_tensor(act_buf[r % 2], ps[:, 2 + r % 2, I:I2], silu_buf[r % 2], ALU.mult).then_inc(s["m_act"], 1)

            def turn_act(i, r, n4):
                v.wait_ge(s["m_aT"], i + 1)
                if not isinstance(i, int) or i >= 2:
                    v.wait_ge(s["m_y_ps"], i - 1)
                v.tensor_copy(actT_buf[r % 2][0:I, :], ps[0:I, 4 + r % 2, 0:P]).then_inc(s["m_actT"], 1)

            def take_y(i, r, n4):
                v.wait_ge(s["m_y_ps"], i + 1)
                if not isinstance(i, int) or i >= 4:
                    v.wait_ge(stored[r], n4 * 16)
                v.tensor_copy(y_buf[r], ps[:, 6 + r % 2, 0:H]).then_inc(s["m_y"], 1)

            skewed(v, [(1, gate_up), (0, turn_act), (-1, take_y)])

            for t in range(NT):
                for k in range(K):
                    n = t * K + k
                    st.add(v.scalar_tensor_tensor(out=rest[:, 3, :], in0=key[:, t, :], scalar=slot8[:, n:n + 1], in1=wdense[:, t, :],
                                                  op0=ALU.is_equal, op1=ALU.mult, accum_out=icol[:, n:n + 1]))
                    st.wait()
                v.wait_ge(picked[t], 16 * K)
                for k in range(K):
                    n = t * K + k
                    ins = v.scalar_tensor_tensor(out=xt[:, t, :], in0=picks[:, n, :], scalar=icol[:, n:n + 1], in1=xt[:, t, :], op0=ALU.mult, op1=ALU.add)
                    if k < K - 1:
                        st.link(ins)
                    else:
                        ins.then_inc(s["out_tile"], 1)

        @block.scalar
        def _(act):
            st = Steps(act, s["act_chain"])
            for i in range(2):
                act.wait_ge(s["ctxT_ps"], i + 1)
                act.copy(ctxT[:, 512 * i:512 * i + 512], bank(i)).then_inc(s["ctxT"], 1)
            act.wait_ge(s["stats"], 1)
            act.activation(rstd, rstd, ACT.Sqrt).then_inc(s["sq"], 1)
            for h in range(NH):
                act.wait_ge(s["xin_ps"], h + 1)
                act.wait_ge(s["consts"], 1)
                act.copy(xin[:, h, :, TAPS - 1:TAPS - 1 + L], bank(4 + 2 * h, 2).rearrange("p (b l) -> p b l", b=B)).then_inc(s["xin"], 1)
            act.wait_ge(loaded["weights"], 16 * 15)
            act.wait_ge(s["qk_ps"], 2)
            act.activation(qT, bank(0, 2), ACT.Identity, bias=bq).then_inc(s["qk"], 1)
            act.activation(kT[:, :], bank(2, 2), ACT.Identity, bias=bk).then_inc(s["qk"], 1)
            act.wait_ge(s["stats"], 2)
            for t in range(NT):
                b, h = t // LT, t % LT
                act.activation(z[:, h, b * L:(b + 1) * L], xt[:, t, :], ACT.Silu, bias=nbias[:, t:t + 1], scale=rstd[:, t:t + 1]).then_inc(s["z_ready"], 1)
            for h in range(NH):
                act.wait_ge(s["conv"], h + 1)
                act.activation(u[:, h, :], conv[h], ACT.Silu).then_inc(s["u_ready"], 1)
            act.wait_ge(loaded["ffn"], 16 * 4)
            for i, raw in enumerate((w1_raw, w2_raw)):
                act.wait_ge(s["u_ready"], NH)
                act.activation(big[:, 4096:6144], raw, ACT.Abs, accum_out=wsum[:, i:i + 1]).then_inc(s["wabs"], 1)
                act.wait_ge(s["wabs"], i + 1)
            st.link(act.activation(Aneg, Aneg, ACT.Exp))
            st.link(act.mul(Aneg, Aneg, -1.0))
            for h in range(NH):
                ab, e = (lb[0], lb[1]) if h == 0 else (lb[3], lb[5])
                act.wait_ge(s["dpre_ps"], h + 1)
                act.wait_ge(s["bc"], 1)
                act.activation(ab, bank(4 + 2 * h, 2), ACT.Abs, bias=dtb[:, h:h + 1]).then_inc(s["xabs"], 1)
                act.wait_ge(s["xabs"], h + 1)
                act.activation(e, ab, ACT.Exp, scale=-1.0).then_inc(s["eneg"], 1)
                act.wait_ge(s["eneg"], h + 1)
                act.activation(delta[:, h, :], e, ACT.Ln, bias=1.0).then_inc(s["lnp"], 1)
            act.wait_ge(s["du_ready"], 2)

            def decay(n):
                h = n // DS
                if n >= 2:
                    act.wait_ge(s["scan"], n - 1)
                act.activation(lb[n % 2].rearrange("p (b l) -> p b l", b=B)[:, :, 1:L],
                               delta[:, h, :].rearrange("p (b l) -> p b l", b=B)[:, :, 1:L],
                               ACT.Exp, scale=Aneg[:, h, n % DS:n % DS + 1]).then_inc(s["dA"], 1)

            decay(0)
            for n in range(STEPS):
                if n + 1 < STEPS:
                    decay(n + 1)
                if n < NT:
                    act.wait_ge(s["att_max"], n + 1)
                    if n >= 2:
                        act.wait_ge(s["attT_ps"], n - 1)
                    act.activation(ex[:, n % 2, :], ps[:, 6, 0:L], ACT.Exp, bias=nmax[:, n:n + 1], accum_out=asum[:, n:n + 1]).then_inc(s["att_exp"], 1)
                if 2 <= n < NT + 2:
                    t = n - 2
                    act.wait_ge(s["attT_ps"], t + 1)
                    act.copy(attT[:, :, t // LT, (t % LT) * P:(t % LT + 1) * P], ps[:, 7, 0:2 * P].rearrange("p (k c) -> p k c", k=LT)).then_inc(s["attT"], 1)
                if n in (22, 24, 26, 28):
                    g = (n - 22) // 2
                    act.wait_ge(s["wqT_ps"], g + 1)
                    dst = w1qT[:, g * FF:(g + 1) * FF] if g < 2 else w2qT[:, :].rearrange("p (k d) -> p k d", k=FK)[:, :, (g - 2) * P:(g - 1) * P]
                    src = bank(6 + g % 2).bitcast(BF16)
                    act.copy(dst, src if g < 2 else src.rearrange("p (k d) -> p k d", k=FK)).then_inc(s["wqT"], 1)

            act.wait_ge(s["ffn_var"], 1)
            act.activation(rstd, rstd, ACT.Sqrt).then_inc(s["ffn_std"], 1)
            act.wait_ge(s["rms_var"], 1)
            act.activation(t8[1], t8[1], ACT.Sqrt).then_inc(s["rms_std"], 1)
            act.wait_ge(s["ffn_norm"], 1)
            for t in range(NT):
                act.activation(xn[:, t, :], xt[:, t, :], ACT.Identity, bias=nbias[:, t:t + 1], scale=rstd[:, t:t + 1]).then_inc(s["xn"], 1)

            def row_sqrt(t):
                act.wait_ge(s["r2_var"], t + 1)
                act.activation(t8[5][:, t:t + 1], t8[5][:, t:t + 1], ACT.Sqrt).then_inc(s["r2_std"], 1)

            for t in range(NT):
                act.wait_ge(s["h_ps"], t + 1)
                if t >= 2:
                    act.wait_ge(s["h_ss"], t - 1)
                act.activation(r_buf[t % 2], bank(2 * (t % 2), 2), ACT.Relu, scale=t8[4][:, t:t + 1]).then_inc(s["h_relu"], 1)
                act.wait_ge(s["h_relu"], t + 1)
                if t >= 2:
                    act.wait_ge(s["hg"], t - 1)
                act.activation(h_buf[t % 2], r_buf[t % 2], ACT.Square).then_inc(s["h_sq"], 1)
                if t >= 1:
                    row_sqrt(t - 1)
                act.wait_ge(s["h_sq"], t + 1)
                act.activation(r_buf[t % 2], h_buf[t % 2], ACT.Square, accum_out=t8[5][:, t:t + 1]).then_inc(s["h_ss"], 1)
            row_sqrt(NT - 1)

            for name, ready in (("at", "x2"), ("ro", "x3")):
                act.wait_ge(s[name + "_var"], 1)
                act.activation(rstd, rstd, ACT.Sqrt).then_inc(s[name + "_std"], 1)
                act.wait_ge(s[name + "_norm"], 1)
                for t in range(NT):
                    if name == "ro":
                        act.wait_ge(s["at_lnT_ps"], NT // 2)
                    act.activation(ln[:, t, :], xt[:, t, :], ACT.Identity, bias=nbias[:, t:t + 1], scale=rstd[:, t:t + 1]).then_inc(s[name + "_ln"], 1)
                for g in range(NT // 2):
                    act.wait_ge(s[name + "_lnT_ps"], g + 1)
                    act.copy(lnT[:, 2 * g:2 * g + 2, :, :].rearrange("p t k c -> p (t k c)"), bank(g)).then_inc(s[name + "_lnT"], 1)
            act.wait_ge(s["logit_shift"], 1)
            act.activation(probs, probs, ACT.Exp).then_inc(s["logit_exp"], 1)

            def take_gT(i, r, n4):
                act.wait_ge(s["m_T"], i + 1)
                if not isinstance(i, int) or i >= 2:
                    act.wait_ge(s["m_h"], i - 1)
                act.copy(gT_buf[r % 2], ps[:, r % 2, 0:H]).then_inc(s["m_gT"], 1)

            def silu(i, r, n4):
                act.wait_ge(s["m_h"], i + 1)
                if not isinstance(i, int) or i >= 2:
                    act.wait_ge(s["m_act"], i - 1)
                act.activation(silu_buf[r % 2], ps[:, 2 + r % 2, 0:I], ACT.Silu).then_inc(s["m_silu"], 1)

            skewed(act, [(2, take_gT), (1, silu)])

        @block.tensor
        def _(pe):
            pe.wait_ge(s["consts"], 1)
            pe.wait_ge(loaded["ctx"], 16)
            for t in range(NT):
                ins = pe.transpose(ps[:, t // 4, (t % 4) * P:(t % 4 + 1) * P], ctx_raw[:, t, :], ident[:])
                if t % 4 == 3:
                    ins.then_inc(s["ctxT_ps"], 1)
            pe.wait_ge(loaded["weights"], 16 * 15)
            for i, w in enumerate((inw_raw[:, 0, :], inw_raw[:, 1, :], wq_raw, wk_raw)):
                ins = pe.transpose(ps[:, 2, i * P:(i + 1) * P], w, ident[:])
            ins.then_inc(s["wT_ps"], 1)
            nx = DR + 2 * DS
            for k in range(NH):
                pe.transpose(ps[:, 3, 64 * k:64 * k + nx], xp_raw[:, k * P:(k + 1) * P], ident[0:nx, 0:nx])
                ins = pe.transpose(ps[0:DR, 3, (k + 1) * P:(k + 2) * P], dt_raw[:, k, :], ident[:])
            ins.then_inc(s["wT_ps"], 1)
            pe.wait_ge(s["ctxT"], 2)
            pe.wait_ge(s["wT"], 1)
            for h in range(NH):
                for c in range(2):
                    ins = pe.matmul(bank(4 + 2 * h + c), wT[:, h * P:(h + 1) * P], ctxT[:, c * 512:(c + 1) * 512], start=True, stop=True)
                ins.then_inc(s["xin_ps"], 1)
            pe.wait_ge(s["wT"], 2)
            for i in range(2):
                for c in range(2):
                    ins = pe.matmul(bank(2 * i + c), wT[:, (2 + i) * P:(3 + i) * P], ctxT[:, c * 512:(c + 1) * 512], start=True, stop=True)
                ins.then_inc(s["qk_ps"], 1)
            pe.wait_ge(s["u_ready"], NH)
            pe.wait_ge(s["qk"], 2)
            for c in range(2):
                for k in range(NH):
                    pe.matmul(ps[0:96, c, :], xpT[:, k, 0:96], u[:, k, c * 512:(c + 1) * 512], start=k == 0, stop=k == NH - 1)
                for k in range(NH):
                    ins = pe.matmul(ps[0:DR, 2 + c, :], xpT[:, k, 96:96 + DR], u[:, k, c * 512:(c + 1) * 512], start=k == 0, stop=k == NH - 1)
            ins.then_inc(s["xdbl_ps"], 1)
            pe.wait_ge(s["dt_lo"], 1)
            pe.wait_ge(s["xin"], NH)
            for h in range(NH):
                for c in range(2):
                    ins = pe.matmul(bank(4 + 2 * h + c), dtT[:, h, :], lb[7][0:DR, c * 512:(c + 1) * 512], start=True, stop=True)
                ins.then_inc(s["dpre_ps"], 1)
            pe.wait_ge(s["bc"], 1)

            def spread(at, row, done):
                for c in range(2):
                    ins = pe.matmul(bank(at + c), sel[:, row:row + 1].broadcast_to([96, P]), bcs[:, c * 512:(c + 1) * 512], start=True, stop=True)
                ins.then_inc(done, 1)

            def energies(t):
                pe.matmul(ps[:, 6, 0:L], qT[:, t * P:(t + 1) * P], kT[:, (t // LT) * L:(t // LT + 1) * L], start=True, stop=True
                          ).then_inc(s["energy"], 1)

            spread(0, 0, s["bmat"])
            spread(2, DS, s["cmat"])
            pe.wait_ge(s["du_ready"], NH)
            energies(0)
            for n in range(STEPS):
                h, i = n // DS, n % 2
                if n + 1 < STEPS:
                    pe.wait_ge(s["dbu"], n + 1)
                    spread(0, (n + 1) % DS, s["bmat"])
                pe.wait_ge(s["hc"], n + 1)
                if n + 1 < STEPS:
                    spread(2, DS + (n + 1) % DS, s["cmat"])
                if n == DS:
                    pe.wait_ge(s["y_ready"], 1)
                for c in range(2):
                    ins = pe.matmul(bank(4 + c), ident[:], lb[6 + i][:, c * 512:(c + 1) * 512], start=n % DS == 0, stop=n % DS == DS - 1)
                ins.then_inc(s["ysum"], 1)
                if n + 1 < NT:
                    pe.wait_ge(s["att_exp"], n + 1)
                    energies(n + 1)
                if 1 <= n <= NT:
                    t = n - 1
                    pe.wait_ge(s["att_norm"], t + 1)
                    if t >= 1:
                        pe.wait_ge(s["attT"], t)
                    for k in range(LT):
                        ins = pe.transpose(ps[:, 7, k * P:(k + 1) * P], ex[:, t % 2, k * P:(k + 1) * P], ident[:])
                    ins.then_inc(s["attT_ps"], 1)
                if n == NT + 1:
                    pe.wait_ge(s["wabs"], 2)
                    pe.wait_ge(s["att_exp"], NT)
                    pe.matmul(ps[:, 6, 0:2], ones, wsum, start=True, stop=True).then_inc(s["wtot"], 1)
                if n in (21, 23, 25, 27):
                    g = (n - 21) // 2
                    pe.wait_ge(s["wquant"], g // 2 + 1)
                    pe.wait_ge(s["wmean_ready"], 1)
                    pe.wait_ge(s["attT"], NT)
                    if g >= 2:
                        pe.wait_ge(s["wqT"], g - 1)
                    dst = bank(6 + g % 2).bitcast(BF16)
                    for j in range(8):
                        if g < 2:
                            src = w1q[:, j * DM + g * P:j * DM + (g + 1) * P]
                        else:
                            src = w2q[:, (g - 2) * FF + j * P:(g - 2) * FF + (j + 1) * P]
                        ins = pe.transpose(dst[:, j * P:(j + 1) * P], src, identb[:])
                    ins.then_inc(s["wqT_ps"], 1)
            pe.wait_ge(s["y_ready"], NH)
            for t in range(NT):
                for h in range(NH):
                    ins = pe.transpose(ps[:, t // 2, ((t % 2) * NH + h) * P:((t % 2) * NH + h + 1) * P], du[:, h, t * P:(t + 1) * P], ident[:])
                if t % 2 == 1:
                    ins.then_inc(s["yT_ps"], 1)

            for t in range(NT):
                pe.wait_ge(s["q1"], t + 1)
                for k in range(KH):
                    ins = pe.transpose(bank(6 + t // 4).bitcast(BF16)[:, ((t % 4) * KH + k) * P:((t % 4) * KH + k + 1) * P], q1[:, t, k * P:(k + 1) * P], identb[:])
                if t % 4 == 3:
                    ins.then_inc(s["q1T_ps"], 1)

            def ffn_up(t):
                pe.wait_ge(s["q1T"], t // 4 + 1)
                pe.wait_ge(s["wqT"], 4)
                pe.wait_ge(s["x1"], NT // 2)
                if t >= 2:
                    pe.wait_ge(s["h_relu"], t - 1)
                for c in range(2):
                    for k in range(KH):
                        ins = pe.matmul(bank(2 * (t % 2) + c), q1T[:, k, t * P:(t + 1) * P], w1T[:, k, c * 512:(c + 1) * 512], start=k == 0, stop=k == KH - 1)
                ins.then_inc(s["h_ps"], 1)

            def ffn_turn(t):
                pe.wait_ge(s["q2"], t + 1)
                if t >= 2:
                    pe.wait_ge(s["q2T"], t - 1)
                for k in range(FK):
                    ins = pe.transpose(bank(4 + t % 2).bitcast(BF16)[:, k * P:(k + 1) * P], q2_buf[t % 2][:, k * P:(k + 1) * P], identb[:])
                ins.then_inc(s["q2T_ps"], 1)

            def ffn_down(t):
                pe.wait_ge(s["q2T"], t + 1)
                pe.wait_ge(s["q1T"], 2)
                if t >= 2:
                    pe.wait_ge(s["x2"], t - 1)
                for k in range(FK):
                    ins = pe.matmul(ps[:, 6 + t % 2, 0:DM], q2T_buf[t % 2][:, k, :], w2T[:, k, :], start=k == 0, stop=k == FK - 1)
                ins.then_inc(s["o_ps"], 1)

            for j in range(NT + 2):
                for off, part_ in ((0, ffn_up), (-1, ffn_turn), (-2, ffn_down)):
                    if 0 <= j + off < NT:
                        part_(j + off)

            def turn_ln(name):
                for t in range(NT):
                    pe.wait_ge(s[name + "_ln"], t + 1)
                    for k in range(KH):
                        ins = pe.transpose(ps[:, t // 2, ((t % 2) * KH + k) * P:((t % 2) * KH + k + 1) * P], ln[:, t, k * P:(k + 1) * P], ident[:])
                    if t % 2 == 1:
                        ins.then_inc(s[name + "_lnT_ps"], 1)

            turn_ln("at")
            pe.wait_ge(s["x2"], NT)
            for t in range(NT):
                pe.wait_ge(s["at_lnT"], t // 2 + 1)
                if t >= 4:
                    pe.wait_ge(s["x3"], t - 3)
                for k in range(LT):
                    ins = pe.matmul(ps[:, 4 + t % 4, 0:L], lnT[:, t, k, :], attT[:, k, t // LT, :], start=k == 0, stop=k == LT - 1)
                ins.then_inc(s["at_ps"], 1)

            turn_ln("ro")
            pe.wait_ge(s["x3"], NT)
            for t in range(NT):
                pe.wait_ge(s["ro_lnT"], t // 2 + 1)
                for k in range(KH):
                    ins = pe.matmul(ps[:, 4, t * E:(t + 1) * E], lnT[:, t, k, :], wgate[:, k, :], start=k == 0, stop=k == KH - 1)
            ins.then_inc(s["logits"], 1)
            pe.wait_ge(s["mask"], 1)
            pe.wait_ge(s["ro_consts"], 1)
            for t in range(NT):
                ins = pe.matmul(ps[:, 6, 0:E], onesb, mask[:, t, :], start=t == 0, stop=t == NT - 1)
            ins.then_inc(s["counts"], 1)
            for t in range(NT):
                for j in range(t):
                    pe.matmul(ps[:, 5, t * E:(t + 1) * E], onesb, mask[:, j, :], start=j == 0, stop=False)
                ins = pe.matmul(ps[:, 5, t * E:(t + 1) * E], before, mask[:, t, :], start=t == 0, stop=True)
            ins.then_inc(s["rank"], 1)
            pe.wait_ge(s["te"], 1)
            pe.transpose(ps[0:1, 7, 0:P], t8[4][:, 0:1], ident[:]).then_inc(s["te_ps"], 1)
            for n in range(NT * K):
                pe.wait_ge(s["onehots"], n + 1)
                pe.matmul(ps[:, 6, 0:P], hot_r[n % RING], hot_i[n % RING], start=n == 0, stop=n == NT * K - 1).then_inc(s["onehots_read"], 1)
            pe.wait_ge(s["onehots_read"], NT * K)
            pe.sem_inc(s["idx_ps"], 1)

            def turn_g(i, r, n4):
                pe.wait_ge(gathered[r], n4 * 16 + 16)
                if not isinstance(i, int) or i >= 2:
                    pe.wait_ge(s["m_gT"], i - 1)
                for k in range(KH):
                    ins = pe.transpose(ps[:, r % 2, k * P:(k + 1) * P], g_buf[r][:, k * P:(k + 1) * P], ident[:])
                ins.then_inc(s["m_T"], 1)

            def up(i, r, n4):
                e = pe.value_load(te_row[0:1, bass.ds(i, 1)] if not isinstance(i, int) else te_row[0:1, i:i + 1], min_val=0, max_val=E - 1)
                pe.wait_ge(s["m_gT"], i + 1)
                if not isinstance(i, int) or i >= 2:
                    pe.wait_ge(s["m_act"], i - 1)
                for k in range(KH):
                    ins = pe.matmul(ps[:, 2 + r % 2, 0:I2], gT_buf[r % 2][:, k * P:(k + 1) * P],
                                    w13[:, bass.ds(e * (KH * I2) + k * I2, I2)], start=k == 0, stop=k == KH - 1)
                ins.then_inc(s["m_h"], 1)

            def turn_act(i, r, n4):
                pe.wait_ge(s["m_act"], i + 1)
                if not isinstance(i, int) or i >= 2:
                    pe.wait_ge(s["m_actT"], i - 1)
                pe.transpose(ps[0:I, 4 + r % 2, 0:P], act_buf[r % 2], ident[:]).then_inc(s["m_aT"], 1)

            def down(i, r, n4):
                e = pe.value_load(te_row[0:1, bass.ds(i, 1)] if not isinstance(i, int) else te_row[0:1, i:i + 1], min_val=0, max_val=E - 1)
                pe.wait_ge(s["m_actT"], i + 1)
                if not isinstance(i, int) or i >= 2:
                    pe.wait_ge(s["m_y"], i - 1)
                pe.matmul(ps[:, 6 + r % 2, 0:H], actT_buf[r % 2][0:I, :], big[0:I, bass.ds(e * H, H)], start=True, stop=True).then_inc(s["m_y_ps"], 1)

            pe.wait_ge(s["te_row"], 1)
            pe.wait_ge(s["idx"], 1)
            pe.wait_ge(loaded["w13"], 16 * (E // EC))
            pe.wait_ge(loaded["w2e"], 16 * 4)
            skewed(pe, [(2, turn_g), (1, up), (0, turn_act), (-1, down)])


_INS = ['x', 'ctx_1024', 'L0_xattn_in_proj_w', 'L0_xattn_conv_w', 'L0_xattn_conv_b', 'L0_xattn_x_proj_w', 'L0_xattn_dt_proj_w',
        'L0_xattn_dt_proj_b', 'L0_xattn_A_log', 'L0_xattn_D', 'L0_ffn_w1', 'L0_ffn_g1', 'L0_ffn_w2', 'L0_ffn_g2',
        'L1_xattn_Wq', 'L1_xattn_bq', 'L1_xattn_Wk', 'L1_xattn_bk', 'L1_ffn_w_gate', 'L1_ffn_w13', 'L1_ffn_w2']


def kernel(**inputs):
    import numpy as _np
    import concourse.bacc as _bacc
    from concourse import mybir as _mybir
    from concourse.bass_utils import run_bass_kernel_spmd as _run

    nc = _bacc.Bacc("TRN2", target_bir_lowering=False, num_devices=1)
    arrays, args = {}, {}
    for name in _INS:
        v = _np.ascontiguousarray(inputs[name])
        arrays[f"in_{name}_dram"] = v
        args[name] = nc.dram_tensor(f"in_{name}_dram", v.shape, _mybir.dt.from_np(v.dtype), kind="ExternalInput").ap()
    out = nc.dram_tensor("out_0_dram", args["x"].shape, F32, kind="ExternalOutput").ap()
    xln_dram = nc.dram_tensor("xln_dram", (1024, 256), F32, kind="Internal").ap()
    y_dram = nc.dram_tensor("y_dram", (128 * 128, 256), F32, kind="Internal").ap()
    mamba_ffn_attention_moe(nc, args, out, xln_dram, y_dram)
    r = _run(nc, [arrays], core_ids=[0])
    return r.results[0]["out_0_dram"]
```

```python
from contextlib import ExitStack

import concourse.bass as bass
from concourse import mybir

ALU = mybir.AluOpType
ACT = mybir.ActivationFunctionType
F32 = mybir.dt.float32
BF16 = mybir.dt.bfloat16
F16 = mybir.dt.float16
I32 = mybir.dt.int32
U32 = mybir.dt.uint32
AX = mybir.AxisListType.X

P = 128
ROUND = 12582912.0


class Steps:

    def __init__(self, engine, sem):
        self.engine, self.sem, self.n = engine, sem, 0

    def add(self, ins):
        self.n += 1
        ins.then_inc(self.sem, 1)
        return self.n

    def wait(self, n=None):
        self.engine.wait_ge(self.sem, self.n if n is None else n)

    def link(self, ins):
        self.add(ins)
        self.wait()


def mamba_ffn_attention_moe(nc, a, out, xln_dram, y_dram):
    B, L, DM = a["x"].shape
    DC = a["ctx_1024"].shape[2]
    DI = a["L0_xattn_in_proj_w"].shape[0]
    NH = DI // P
    DS = a["L0_xattn_A_log"].shape[1]
    TAPS = a["L0_xattn_conv_w"].shape[1]
    DR = a["L0_xattn_dt_proj_w"].shape[1]
    FF = a["L0_ffn_w1"].shape[0]
    E, H, I2 = a["L1_ffn_w13"].shape
    I = I2 // 2
    K = 8
    T = B * L
    NT = T // P
    LT = L // P
    KH = H // P
    FK = FF // P
    MT = T * K // P + E
    STEPS = NH * DS
    GATHERS = 12
    STORES = 4
    UNROLL = 2 * GATHERS

    with ExitStack() as ctx:
        def sb(name, shape, dt=F32):
            return ctx.enter_context(nc.sbuf_tensor(name, shape, dt))

        def sem(name):
            return ctx.enter_context(nc.semaphore(name))

        EC = 4
        LATE = 20
        w13 = sb("w13", [P, E * KH * I2])
        w13e = w13[:, :].rearrange("p (e k d) -> p e k d", e=E, k=KH)
        late = w13[:, (E - LATE) * KH * I2:]
        big = sb("big", [P, 16384])
        area = sb("area", [P, 6400])
        xt = sb("xt", [P, NT, DM])
        ctxT = sb("ctxT", [P, T])
        attT = late[:, 0:2048].rearrange("p (k b m) -> p k b m", k=LT, b=B)
        w1qT = late[:, 2048:3072].bitcast(BF16)
        w2qT = late[:, 3072:4096].bitcast(BF16)
        bsb = [late[:, 4096 + 1024 * i:5120 + 1024 * i] for i in range(2)]
        ident = sb("ident", [P, P])
        identb = sb("identb", [P, P], BF16)
        g1 = sb("g1", [P, DM])
        g2 = sb("g2", [P, FF])
        wgate = sb("wgate", [P, KH, E])
        small = sb("small", [P, 620])
        ps = ctx.enter_context(nc.psum_tensor("ps", [P, 8, 512], F32))

        def bank(i, n=1):
            return ps[:, i:i + n, :].rearrange("p a c -> p (a c)")

        def part(t, at, n, dt=F32):
            v = t[:, at:at + n]
            return v if dt == F32 else v.bitcast(dt)

        u = part(big, 0, 2048).rearrange("p (h t) -> p h t", h=NH)
        delta = part(big, 2048, 2048).rearrange("p (h t) -> p h t", h=NH)
        du = part(big, 4096, 2048).rearrange("p (h t) -> p h t", h=NH)
        z = part(big, 6144, 2048).rearrange("p (h t) -> p h t", h=NH)
        lb = [part(big, 8192 + 1024 * i, 1024) for i in range(8)]
        ctx_raw = lb[0].rearrange("p (t c) -> p t c", t=NT)
        inw_raw = lb[1][:, 0:256].rearrange("p (h c) -> p h c", h=NH)
        wq_raw, wk_raw = lb[1][:, 256:384], lb[1][:, 384:512]
        xp_raw = lb[1][0:DR + 2 * DS, 512:768]
        dt_raw = lb[1][:, 768:784].rearrange("p (h r) -> p h r", h=NH)
        conv = [lb[2], lb[3]]
        w2e = big[0:I, :].rearrange("p (e d) -> p e d", e=E)
        w1_raw = part(area, 0, 2048)
        w2_raw = part(area, 2048, 2048)
        xin = part(area, 4096, NH * B * (L + TAPS - 1)).rearrange("p (h b l) -> p h b l", h=NH, b=B)
        w1q, w2q = (b.bitcast(BF16) for b in bsb)
        cw = small[:, 0:8].rearrange("p (h k) -> p h k", h=NH)
        cb, dtb, dsk = small[:, 8:10], small[:, 10:12], small[:, 12:14]
        bq, bk = small[:, 14:15], small[:, 15:16]
        Aneg = small[:, 16:48].rearrange("p (h n) -> p h n", h=NH)
        mv = small[:, 48:64].rearrange("p (t s) -> p t s", t=NT)
        rstd, nbias = small[:, 64:72], small[:, 72:80]
        stat = small[:, 80:128].rearrange("p (t s) -> p t s", t=NT)
        sel = small[0:96, 128:144].bitcast(BF16)
        wsum, wmean, wscale = small[:, 144:146], small[:, 146:148], small[:, 148:150]
        nmax, asum, arec = small[:, 152:160], small[:, 160:168], small[:, 168:176]
        xpT = small[:, 176:368].rearrange("p (k c) -> p k c", k=NH)
        ones = small[:, 384:512]
        t8 = [small[:, 512 + 8 * i:520 + 8 * i] for i in range(13)]

        bcs = g2[0:96, 0:512].bitcast(BF16)
        dtT = lb[7][0:DR, 0:DI]
        dtxT = lb[7][:, 256:768].rearrange("p (k e) -> p k e", k=NH)
        ex = g2[:, 512:1024].rearrange("p (i l) -> p i l", i=2)
        wT = w2qT[:, 0:1024].bitcast(F32)
        qT = late[:, 6144:7168]
        kT = ctxT

        loaded = {n: sem("loaded_" + n) for n in ("ctx", "proj", "vectors", "x", "ffn", "g2", "w13", "w2e")}
        names = ("consts ctxT_ps ctxT wT_ps wT dtxT_ps dtxT xin_ps xin conv u_ready qk_ps qk bc_ps bc_hi bc dpre_ps xabs relu eneg lnp delta_ready "
                 "du_first du_ready z_ready bmat b_copied cmat dA dbu scan hc sequence_starts ysum y_ready yT_ps x1 "
                 "energy att_max att_exp att_norm attT_ps attT wabs wtot wmean_ready wquant wqT_ps wqT "
                 "dve_chain act_chain pool_chain stats sq stored_out "
                 "ffn_var ffn_std ffn_scale xn q1 q1T_ps q1T h_ps h_relu h_sq h_ss hg r2_var r2_std q2 q2T_ps q2T o_ps x2 "
                 "at_var at_std at_ln at_lnT_ps at_lnT at_ps x3 ro_var ro_std ro_ln ro_lnT_ps ro_lnT ro_consts "
                 "logits logit_shift logit_exp mask rank counts te te_ps te_row slots onehots row_diffs row_onehots onehots_read idx_ps idx xln_stored "
                 "m_T m_gT m_h m_silu m_act m_aT m_actT m_y_ps m_y out_tile").split()
        s = {n: sem(n) for n in names}
        gathered = [sem(f"gathered{r}") for r in range(GATHERS)]
        stored = [sem(f"stored{r}") for r in range(STORES)]
        picked = [sem(f"picked{t}") for t in range(NT - 1)]
        picked_last = [sem(f"picked_last{k}") for k in range(K)]

        r_buf = [part(big, 1024 * i, 1024) for i in range(2)]
        h_buf = [part(big, 2048 + 1024 * i, 1024) for i in range(2)]
        hg_buf = [part(big, 4096 + 1024 * i, 1024) for i in range(2)]
        q2_buf = [part(big, 6144 + 512 * i, 512, BF16) for i in range(2)]
        q2T_buf = [part(big, 7168 + 512 * i, 512, BF16).rearrange("p (k c) -> p k c", k=FK) for i in range(2)]
        xn = part(big, 8192, 2048).rearrange("p (t d) -> p t d", t=NT)
        q1 = part(big, 10240, 1024, BF16).rearrange("p (t d) -> p t d", t=NT)
        q1T = part(big, 11264, 1024, BF16).rearrange("p (k t) -> p k t", k=KH)
        w1T = w1qT.rearrange("p (k f) -> p k f", k=KH)
        w2T = w2qT.rearrange("p (k d) -> p k d", k=FK)
        ln = part(area, 0, 2048).rearrange("p (t d) -> p t d", t=NT)
        lnT = part(area, 2048, 2048).rearrange("p (t k c) -> p t k c", t=NT, k=KH)
        wdense = part(area, 5248, 512).rearrange("p (t e) -> p t e", t=NT)
        key = part(area, 5760, 512).rearrange("p (t e) -> p t e", t=NT)
        probs = g2[:, 0:512].rearrange("p (t e) -> p t e", t=NT)
        rest = g2[:, 512:1024].rearrange("p (t e) -> p t e", t=NT)
        mask = ctxT[:, 0:256].bitcast(BF16).rearrange("p (t e) -> p t e", t=NT)
        iota = ctxT[:, 256:320].bitcast(F16)
        DVE_ROWS = 2
        POOL_RING = 5
        hot_row = [part(area, 2048 + 512 * i, 512, F16).rearrange("p (k c) -> p k c", k=K) for i in range(DVE_ROWS + POOL_RING)]
        hot_tile = [part(area, 512 * i, 512, F16).rearrange("p (k c) -> p k c", k=K) for i in range(4)]
        row16, tile16 = ctxT[:, 320:352].bitcast(F16), ctxT[:, 352:384].bitcast(F16)
        before = ctxT[:, 832:896].bitcast(BF16)
        onesb = ctxT[:, 896:960].bitcast(BF16)

        def spread_out(numbers, t):
            return (iota.unsqueeze(1).broadcast_to([P, K, P]), numbers[:, K * t:K * t + K].unsqueeze(2).broadcast_to([P, K, P]))

        idx = g1[:, 0:128].bitcast(U32)
        slot = g1[:, 128:192].bitcast(U32)
        slot8 = g1[:, 192:256]
        ntile, tend, base = small[:, 176:240], small[:, 240:304], small[:, 304:368]
        te_row = wgate[0:1, :, :].rearrange("p k e -> p (k e)").bitcast(I32)
        icol = ctxT[:, 960:1024]
        g_buf = [part(area, 256 * i, 256) for i in range(GATHERS)]
        gT_buf = [part(area, 3072 + 256 * i, 256) for i in range(2)]
        silu_buf = [part(area, 3584 + 96 * i, 96) for i in range(2)]
        act_buf = [part(area, 3776 + 96 * i, 96) for i in range(2)]
        actT_buf = [part(area, 3968 + 128 * i, 128) for i in range(2)]
        y_buf = [part(area, 4224 + 256 * i, 256) for i in range(STORES)]
        unused = w13[:, NT * K * DM:NT * K * (DM + E)].rearrange("p (n e) -> p n e", e=E)
        picks = w13[:, 0:NT * K * DM].rearrange("p (s d) -> p s d", s=NT * K)

        def first_free(i, ring):
            return not isinstance(i, int) or i >= ring

        def skewed(engine, parts):
            first = 5
            loops = (MT - 2 - first) // UNROLL

            def body(j):
                for lag, part_ in parts:
                    i = j + lag
                    if 0 <= i < MT:
                        part_(i, i % UNROLL, i // UNROLL)

            for j in range(-2, first):
                body(j)
            with engine.Fori(0, loops) as q:
                for c in range(UNROLL):
                    for lag, part_ in parts:
                        i0 = first + c + lag
                        part_(q * UNROLL + i0, i0 % UNROLL, q + i0 // UNROLL)
            for j in range(first + loops * UNROLL, MT + 1):
                body(j)

        block = ctx.enter_context(nc.Block())

        @block.sync
        def _(sp):
            sp.dma_start(ctx_raw, a["ctx_1024"].rearrange("b (h p) d -> p (b h) d", p=P)).then_inc(loaded["ctx"], 16)
            for dst, src in (
                (inw_raw, a["L0_xattn_in_proj_w"].rearrange("(h p) c -> p h c", p=P)),
                (wq_raw, a["L1_xattn_Wq"]), (wk_raw, a["L1_xattn_Wk"]),
                (xp_raw, a["L0_xattn_x_proj_w"]),
                (dt_raw, a["L0_xattn_dt_proj_w"].rearrange("(h p) r -> p h r", p=P)),
            ):
                sp.dma_start(dst, src).then_inc(loaded["proj"], 16)
            sp.dma_start(xt[:], a["x"].rearrange("b (h p) d -> p (b h) d", p=P)).then_inc(loaded["x"], 16)
            for dst, src in (
                (w1_raw.rearrange("p (j c) -> p j c", j=FK), a["L0_ffn_w1"].rearrange("(j p) c -> p j c", p=P)),
                (w2_raw.rearrange("p (h f) -> p h f", h=NH), a["L0_ffn_w2"].rearrange("(h p) f -> p h f", p=P)),
                (g1[:], a["L0_ffn_g1"].partition_broadcast(P)),
                (wgate[:], a["L1_ffn_w_gate"].rearrange("(k p) e -> p k e", p=P)),
            ):
                sp.dma_start(dst, src).then_inc(loaded["ffn"], 16)

            def load_w13(e):
                sp.dma_start(w13e[:, e:e + EC, :, :].rearrange("p e k d -> p (e k) d"), a["L1_ffn_w13"][e:e + EC].rearrange("e (k p) d -> p (e k) d", p=P)
                             ).then_inc(loaded["w13"], 16)

            sp.wait_ge(loaded["vectors"], 16 * 10)
            for e in range(0, E - LATE, EC):
                load_w13(e)
            sp.wait_ge(s["x1"], NT // 2)
            sp.dma_start(g2[:], a["L0_ffn_g2"].partition_broadcast(P)).then_inc(loaded["g2"], 16)

            def load_w2(e):
                sp.dma_start(w2e[:, e:e + 16, :], a["L1_ffn_w2"][e:e + 16].rearrange("e p d -> p e d")).then_inc(loaded["w2e"], 16)

            load_w2(48)
            sp.wait_ge(s["h_ps"], NT)
            load_w2(32)
            sp.wait_ge(s["x2"], NT)
            load_w2(0)
            load_w2(16)
            sp.wait_ge(s["ro_ln"], NT)
            sp.dma_start(xln_dram.rearrange("(t p) d -> p t d", p=P), ln).then_inc(s["xln_stored"], 16)
            sp.wait_ge(s["x3"], NT)
            for e in range(E - LATE, E, EC):
                load_w13(e)

            def store(i, n, turn):
                sp.wait_ge(s["m_y"], i + 1)
                sp.dma_start(y_dram[bass.ds(i * P, P), :], y_buf[n % STORES]).then_inc(stored[n % STORES], 16)

            skewed(sp, [(-1, store)])
            for t in range(NT):
                sp.wait_ge(s["out_tile"], t + 1)
                sp.dma_start(out.rearrange("b (h p) d -> p (b h) d", p=P)[:, t, :], xt[:, t, :]).then_inc(s["stored_out"], 16)
            sp.wait_ge(s["stored_out"], 16 * NT)

        @block.gpsimd
        def _(pool):
            st = Steps(pool, s["pool_chain"])
            st.add(pool.memset(ident[:], 0.0))
            st.add(pool.memset(identb[:], 0.0))
            st.add(pool.memset(sel, 0.0))
            st.add(pool.memset(ones, 1.0))
            st.add(pool.memset(xin[:, :, :, 0:TAPS - 1], 0.0))
            st.wait()
            st.link(pool.affine_select(out=ident[:], in_=ident[:], compare_op=ALU.not_equal, fill=1.0, base=0, pattern=[[-1, P]], channel_multiplier=1))
            st.link(pool.affine_select(out=identb[:], in_=identb[:], compare_op=ALU.not_equal, fill=1.0, base=0, pattern=[[-1, P]], channel_multiplier=1))
            for g in range(3):
                st.link(pool.affine_select(out=sel, in_=sel, compare_op=ALU.not_equal, fill=1.0, base=-32 * g, pattern=[[-1, 32]], channel_multiplier=1))
            pool.sem_inc(s["consts"], 1)
            for dst, src in (
                (cw, a["L0_xattn_conv_w"].rearrange("(h p) k -> p h k", p=P)),
                *((dst[:, h:h + 1], a["L0_xattn_" + n][h * P:(h + 1) * P].rearrange("(p o) -> p o", o=1))
                  for dst, n in ((cb, "conv_b"), (dtb, "dt_proj_b"), (dsk, "D")) for h in range(NH)),
                (bq, a["L1_xattn_bq"].rearrange("(p o) -> p o", o=1)),
                (bk, a["L1_xattn_bk"].rearrange("(p o) -> p o", o=1)),
                (Aneg, a["L0_xattn_A_log"].rearrange("(h p) n -> p h n", p=P)),
            ):
                pool.dma_start(dst, src).then_inc(loaded["vectors"], 16)

            pool.wait_ge(s["wmean_ready"], 1)
            for i, (raw, q) in enumerate(((w1_raw, w1q), (w2_raw, w2q))):
                st.link(pool.tensor_scalar(raw, raw, wscale[:, i:i + 1], ROUND, ALU.mult, ALU.add))
                pool.tensor_scalar(q, raw, -ROUND, 1.0, ALU.add, ALU.mult).then_inc(s["wquant"], 1)
            pool.wait_ge(s["delta_ready"], 1)
            pool.tensor_tensor(du[:, :, 0:512], delta[:, :, 0:512], u[:, :, 0:512], ALU.mult).then_inc(s["du_first"], 1)
            pool.wait_ge(s["du_first"], 1)
            pool.wait_ge(s["du_ready"], 1)
            for m in range(STEPS):
                n, h = m // NH, m % NH
                pool.wait_ge(s["b_copied"], n + 1)
                if m >= 2:
                    pool.wait_ge(s["scan"], m - 1)
                pool.tensor_tensor(lb[2 + h], bsb[n % 2], du[:, h, :], ALU.mult).then_inc(s["dbu"], 1)
            st.add(pool.iota(iota, [[1, P]], base=0, channel_multiplier=0, allow_small_or_imprecise_dtypes=True))
            st.add(pool.iota(t8[0], [[P, NT]], base=0, channel_multiplier=1, allow_small_or_imprecise_dtypes=True))
            st.link(pool.memset(onesb, 1.0))
            pool.affine_select(out=before, in_=onesb, compare_op=ALU.is_gt, fill=0.0, base=0, pattern=[[1, P]], channel_multiplier=-1).then_inc(s["ro_consts"], 1)
            pool.wait_ge(loaded["g2"], 16)
            for t in range(NT):
                pool.wait_ge(s["h_sq"], t + 1)
                if t >= 2:
                    pool.wait_ge(s["q2"], t - 1)
                pool.tensor_tensor(hg_buf[t % 2], h_buf[t % 2], g2[:], ALU.mult).then_inc(s["hg"], 1)
            pool.wait_ge(s["slots"], 1)
            for t in range(DVE_ROWS, NT):
                i = t - DVE_ROWS
                if i >= POOL_RING:
                    pool.wait_ge(s["onehots_read"], t - POOL_RING + 1)
                pool.tensor_tensor(hot_row[DVE_ROWS + i % POOL_RING], *spread_out(row16, t), ALU.subtract).then_inc(s["row_diffs"], 1)
            pool.wait_ge(s["idx"], 1)
            pool.wait_ge(s["xln_stored"], 16)
            for i in range(MT):
                if i >= GATHERS:
                    pool.wait_ge(s["m_T"], i - GATHERS + 1)
                pool.indirect_dma_start(g_buf[i % GATHERS], None, xln_dram, bass.IndirectOffsetOnAxis(ap=idx[:, i:i + 1], axis=0)
                                        ).then_inc(gathered[i % GATHERS], 16)
            for r in range(STORES):
                pool.wait_ge(stored[r], 16 * (MT // STORES))
            for n in range(NT * K):
                pool.indirect_dma_start(picks[:, n, :], None, y_dram, bass.IndirectOffsetOnAxis(ap=slot[:, n:n + 1], axis=0)
                                        ).then_inc(picked[n // K] if n // K < NT - 1 else picked_last[n % K], 16)

        @block.vector
        def _(v):
            st = Steps(v, s["dve_chain"])
            v.wait_ge(s["wT_ps"], 1)
            v.tensor_copy(wT, bank(2)).then_inc(s["wT"], 1)
            v.wait_ge(s["wT_ps"], 2)
            raw = ps[:, 3, 0:128].rearrange("p (k c) -> p k c", k=NH)
            for g in range(3):
                st.add(v.tensor_copy(xpT[:, :, 32 * g:32 * g + 32], raw[:, :, DR:DR + 32]))
            v.tensor_copy(dtT, ps[0:DR, 3, 128:384]).then_inc(s["wT"], 1)
            st.wait()
            v.wait_ge(loaded["x"], 16)
            done = [st.add(v.bn_stats(stat[:, t, :], xt[:, t, :])) for t in range(NT)]
            for t in range(NT):
                st.wait(done[t])
                last = st.add(v.bn_aggr(mv[:, t, :], stat[:, t, :]))
            st.wait(last)
            v.tensor_scalar(rstd, mv[:, :, 1], 1e-5, None, ALU.add).then_inc(s["stats"], 1)
            v.wait_ge(s["dtxT_ps"], 1)
            v.tensor_copy(dtxT, ps[:, 2, :].rearrange("p (k e) -> p k e", k=NH)).then_inc(s["dtxT"], 1)

            v.wait_ge(loaded["vectors"], 16 * 10)
            for c in range(2):
                for k in range(TAPS):
                    for h in range(NH):
                        if c == 0 and k == 0:
                            v.wait_ge(s["xin"], h + 1)
                        cv = conv[h].rearrange("p (b l) -> p b l", b=B)[:, 2 * c:2 * c + 2, :]
                        src = xin[:, h, 2 * c:2 * c + 2, TAPS - 1 - k:TAPS - 1 - k + L]
                        w = cw[:, h, TAPS - 1 - k:TAPS - k]
                        if k == 0:
                            ins = v.tensor_scalar(cv, src, w, cb[:, h:h + 1], ALU.mult, ALU.add)
                        else:
                            st.wait(prev[h])
                            ins = v.scalar_tensor_tensor(out=cv, in0=src, scalar=w, in1=cv, op0=ALU.mult, op1=ALU.add)
                        if k == TAPS - 1:
                            ins.then_inc(s["conv"], 1)
                        else:
                            if k == 0 and h == 0:
                                prev = {}
                            prev[h] = st.add(ins)
                if c == 0:
                    v.wait_ge(s["sq"], 1)
                    st.link(v.reciprocal(rstd, rstd))
                    v.scalar_tensor_tensor(out=nbias, in0=mv[:, :, 0], scalar=-1.0, in1=rstd, op0=ALU.mult, op1=ALU.mult).then_inc(s["stats"], 1)
                    v.wait_ge(s["wtot"], 1)
                    st.link(v.tensor_scalar(wmean, ps[:, 4, 0:2], 1.0 / (FF * DM), 1e-5, ALU.mult, ALU.max))
                    v.reciprocal(wscale, wmean).then_inc(s["wmean_ready"], 1)

            for i, (dst, bias) in enumerate(((qT, bq), (kT[:, :], bk))):
                v.wait_ge(s["qk_ps"], i + 1)
                v.tensor_scalar(dst, bank(2 * i, 2), bias, None, ALU.add).then_inc(s["qk"], 1)

            def halves(t, c):
                return t[:, :, 512 * c:512 * c + 512]

            bc, r1 = bank(0, 2)[0:96, :], lb[5][0:96, :]

            def split_bc():
                v.wait_ge(s["bc_hi"], 1)
                st.link(v.tensor_tensor(r1, bc, bcs, ALU.subtract))
                st.add(v.tensor_copy(bcs[32:64, :], r1[32:64, :]))
                st.link(v.tensor_copy(bcs[64:96, :], r1[64:96, :]))
                v.tensor_tensor(bcs[64:96, :], r1[64:96, :], bcs[64:96, :], ALU.subtract).then_inc(s["bc"], 1)

            for c in range(2):
                v.wait_ge(s["eneg"], c + 1)
                e, w = lb[0 + c].rearrange("p (h t) -> p h t", h=NH), lb[2 + c].rearrange("p (h t) -> p h t", h=NH)
                st.link(v.tensor_scalar(w, e, 1.0, None, ALU.add))
                st.link(v.scalar_tensor_tensor(out=w, in0=w, scalar=-1.0, in1=e, op0=ALU.add, op1=ALU.subtract))
                v.wait_ge(s["relu"], NH * c + NH)
                st.link(v.tensor_tensor(w, halves(du, c), w, ALU.subtract))
            split_bc()
            for c in range(2):
                v.wait_ge(s["lnp"], c + 1)
                v.tensor_tensor(halves(delta, c), halves(delta, c), lb[2 + c].rearrange("p (h t) -> p h t", h=NH), ALU.add).then_inc(s["delta_ready"], 1)
            for i in range(2):
                st.add(v.memset(lb[i].rearrange("p (b l) -> p b l", b=B)[:, :, 0:1], 0.0))
            st.wait()
            v.sem_inc(s["sequence_starts"], 1)
            v.wait_ge(s["delta_ready"], 2)
            v.tensor_tensor(halves(du, 1), halves(delta, 1), halves(u, 1), ALU.mult).then_inc(s["du_ready"], 1)

            def finish_y(h, cols):
                v.wait_ge(s["ysum"], STEPS - 1 + h)
                v.wait_ge(s["z_ready"], NT)
                st.link(v.scalar_tensor_tensor(out=u[:, h, cols], in0=u[:, h, cols], scalar=dsk[:, h:h + 1], in1=bank(4 + 2 * h, 2)[:, cols], op0=ALU.mult, op1=ALU.add))
                v.tensor_tensor(du[:, h, cols], u[:, h, cols], z[:, h, cols], ALU.mult).then_inc(s["y_ready"], 1)

            for m in range(STEPS):
                n, h = m // NH, m % NH
                v.wait_ge(s["dbu"], m + 1)
                v.wait_ge(s["dA"], m + 1)
                v.tensor_tensor_scan(lb[4 + h], lb[h], lb[2 + h], 0.0, ALU.mult, ALU.add).then_inc(s["scan"], 1)
                v.wait_ge(s["scan"], m + 1)
                v.wait_ge(s["cmat"], n + 1)
                if m >= 2:
                    v.wait_ge(s["ysum"], m - 1)
                v.tensor_tensor(lb[6 + h], bank(2, 2), lb[4 + h], ALU.mult).then_inc(s["hc"], 1)
                if h == 0 and 1 <= n <= NT:
                    v.wait_ge(s["att_exp"], n)
                    st.link(v.reciprocal(arec[:, n - 1:n], asum[:, n - 1:n]))
                    v.tensor_scalar(ex[:, (n - 1) % 2, :], ex[:, (n - 1) % 2, :], arec[:, n - 1:n], None, ALU.mult).then_inc(s["att_norm"], 1)
                if h == 1 and n < NT:
                    v.wait_ge(s["energy"], n + 1)
                    v.tensor_reduce(nmax[:, n:n + 1], ps[:, 0, 0:L], AX, ALU.max, negate=True).then_inc(s["att_max"], 1)
            finish_y(0, slice(0, T))
            for c in range(2):
                finish_y(1, slice(512 * c, 512 * c + 512))

            bn = {}

            def take_stats(sem_, need, t):
                v.wait_ge(sem_, need)
                bn[t] = st.add(v.bn_stats(stat[:, t, :], xt[:, t, :]))

            def variance(c, a1, a2, var):
                for t in range(NT)[c]:
                    st.wait(bn[t])
                    last_ = st.add(v.bn_aggr(mv[:, t, :], stat[:, t, :]))
                st.wait(last_)
                v.tensor_scalar(rstd[:, c], mv[:, c, 1], a1, a2, ALU.mult, ALU.add).then_inc(s[var], 1)

            def norm(c, std, n, done_):
                v.wait_ge(s[std], n)
                st.link(v.reciprocal(rstd[:, c], rstd[:, c]))
                for t in range(NT)[c]:
                    v.tensor_scalar(ln[:, t, :], xt[:, t, :], mv[:, t, 0:1], rstd[:, t:t + 1], ALU.subtract, ALU.mult).then_inc(s[done_], 1)

            HALF = NT // 2
            tiles = [slice(0, HALF), slice(HALF, NT)]

            def mamba_added(g):
                for q in (2 * g, 2 * g + 1):
                    v.wait_ge(s["yT_ps"], q + 1)
                    v.tensor_tensor(xt[:, 2 * q:2 * q + 2, :].rearrange("p t c -> p (t c)"), bank(q),
                                    xt[:, 2 * q:2 * q + 2, :].rearrange("p t c -> p (t c)"), ALU.add).then_inc(s["x1"], 1)
                for t in range(NT)[tiles[g]]:
                    take_stats(s["x1"], t // 2 + 1, t)

            amax, qs, oscale, f = t8[2], t8[3], t8[4], t8[1]

            def scaled(g):
                c = tiles[g]
                variance(c, 1.0 + 1e-6, 1e-11, "ffn_var")
                if g == 1:
                    turned(0)
                for t in range(NT)[c]:
                    st.add(v.scalar_tensor_tensor(out=xn[:, t, :], in0=xt[:, t, :], scalar=mv[:, t, 0:1], in1=g1[:], op0=ALU.subtract, op1=ALU.mult))
                st.wait()
                st.link(v.tensor_reduce(amax[:, c], xn[:, c, :], AX, ALU.max, apply_absolute_value=True))
                v.wait_ge(s["ffn_std"], g + 1)
                st.link(v.reciprocal(rstd[:, c], rstd[:, c]))
                st.link(v.tensor_tensor(amax[:, c], amax[:, c], rstd[:, c], ALU.mult))
                st.link(v.tensor_scalar(amax[:, c], amax[:, c], 1e-5, None, ALU.max))
                st.link(v.reciprocal(qs[:, c], amax[:, c]))
                st.link(v.tensor_scalar(qs[:, c], qs[:, c], 127.0, None, ALU.mult))
                v.tensor_tensor(f[:, c], qs[:, c], rstd[:, c], ALU.mult).then_inc(s["ffn_scale"], 1)
                st.add(v.tensor_scalar(oscale[:, c], amax[:, c], 1.0 / 127.0, wmean[:, 0:1], ALU.mult, ALU.mult))

            def rounded(g):
                v.wait_ge(s["xn"], HALF * (g + 1))
                v.tensor_scalar(q1[:, tiles[g], :], xn[:, tiles[g], :], ROUND, -ROUND, ALU.add, ALU.add).then_inc(s["q1"], 1)

            def turned(g):
                v.wait_ge(s["q1T_ps"], g + 1)
                if g == 1:
                    st.wait()
                v.tensor_scalar(q1T[:, :, 512 * g:512 * g + 512].rearrange("p k (t c) -> p t k c", t=4),
                                bank(6 + g).bitcast(BF16).rearrange("p (t k c) -> p t k c", t=4, k=KH), -128.0, 127.0, ALU.max, ALU.min).then_inc(s["q1T"], 1)

            mamba_added(0)
            scaled(0)
            mamba_added(1)
            rounded(0)
            scaled(1)
            rounded(1)
            turned(1)

            def ffn_quant(t):
                c = slice(t, t + 1)
                v.wait_ge(s["r2_std"], t + 1)
                st.link(v.reciprocal(t8[5][:, c], t8[5][:, c]))
                st.link(v.tensor_scalar(t8[6][:, c], t8[6][:, c], t8[5][:, c], 1e-5, ALU.mult, ALU.max))
                st.link(v.reciprocal(t8[7][:, c], t8[6][:, c]))
                st.link(v.tensor_scalar(t8[7][:, c], t8[7][:, c], 127.0, t8[5][:, c], ALU.mult, ALU.mult))
                st.add(v.tensor_scalar(hg_buf[t % 2], hg_buf[t % 2], t8[7][:, c], ROUND, ALU.mult, ALU.add))
                st.link(v.tensor_scalar(t8[8][:, c], t8[6][:, c], 1.0 / 127.0, wmean[:, 1:2], ALU.mult, ALU.mult))
                if t >= 2:
                    v.wait_ge(s["q2T_ps"], t - 1)
                v.tensor_scalar(q2_buf[t % 2], hg_buf[t % 2], -ROUND, 127.0, ALU.add, ALU.min).then_inc(s["q2"], 1)

            def ffn_max(t):
                v.wait_ge(s["hg"], t + 1)
                st.add(v.tensor_reduce(t8[6][:, t:t + 1], hg_buf[t % 2], AX, ALU.max, apply_absolute_value=True))

            def ffn_var(t):
                v.wait_ge(s["h_ss"], t + 1)
                v.tensor_scalar(t8[5][:, t:t + 1], t8[5][:, t:t + 1], 1.0 / FF, 1e-6, ALU.mult, ALU.add).then_inc(s["r2_var"], 1)

            def ffn_add(t):
                v.wait_ge(s["o_ps"], t + 1)
                st.wait()
                v.scalar_tensor_tensor(out=xt[:, t, :], in0=ps[:, 6 + t % 2, 0:DM], scalar=t8[8][:, t:t + 1], in1=xt[:, t, :], op0=ALU.mult, op1=ALU.add).then_inc(s["x2"], 1)

            def ffn_stats(t):
                take_stats(s["x2"], t + 1, t)
                if t % HALF == HALF - 1:
                    variance(tiles[t // HALF], 1.0, 1e-5, "at_var")

            for j in range(NT + 5):
                for off, part_ in ((-1, ffn_quant), (0, ffn_var), (0, ffn_max), (-4, ffn_add), (-5, ffn_stats)):
                    if 0 <= j + off < NT:
                        part_(j + off)
                if j - 5 == HALF:
                    norm(tiles[0], "at_std", 1, "at_ln")

            norm(tiles[1], "at_std", 2, "at_ln")
            for t in range(NT + 1):
                if t < NT:
                    v.wait_ge(s["at_ps"], t + 1)
                    v.tensor_tensor(xt[:, t, :], ps[:, 4 + t % 4, 0:L], xt[:, t, :], ALU.add).then_inc(s["x3"], 1)
                if t >= 1:
                    take_stats(s["x3"], t, t - 1)
                if t == HALF:
                    variance(tiles[0], 1.0, 1e-5, "ro_var")
            v.wait_ge(s["at_lnT_ps"], NT // 2)
            norm(tiles[0], "ro_std", 1, "ro_ln")
            variance(tiles[1], 1.0, 1e-5, "ro_var")
            norm(tiles[1], "ro_std", 2, "ro_ln")

            logits = [ps[:, 4 + 3 * g, 0:HALF * E].rearrange("p (t e) -> p t e", t=HALF) for g in range(2)]

            def wide(col):
                return col.unsqueeze(2).broadcast_to([P, HALF, E])

            for g, c in enumerate(tiles):
                v.wait_ge(s["logits"], g + 1)
                st.link(v.tensor_reduce(t8[1][:, c], logits[g], AX, ALU.max))
                v.tensor_tensor(probs[:, c, :], logits[g], wide(t8[1][:, c]), ALU.subtract).then_inc(s["logit_shift"], 1)
            for g, c in enumerate(tiles):
                v.wait_ge(s["logit_exp"], g + 1)
                st.link(v.tensor_reduce(t8[2][:, c], probs[:, c, :], AX, ALU.add))
                st.link(v.reciprocal(t8[2][:, c], t8[2][:, c]))
                st.link(v.tensor_tensor(probs[:, c, :], probs[:, c, :], wide(t8[2][:, c]), ALU.mult))
                top = [st.add(v.max(out=slot8[:, K * t:K * t + K], in_=probs[:, t, :])) for t in range(NT)[c]]
                for t, done in zip(range(NT)[c], top):
                    st.wait(done)
                    st.add(v.match_replace(rest[:, t, :], slot8[:, K * t:K * t + K], probs[:, t, :], -1.0))
                st.wait()
                v.tensor_scalar(mask[:, c, :], rest[:, c, :], 0.0, None, ALU.is_lt).then_inc(s["mask"], 1)
            st.link(v.tensor_reduce(t8[3], slot8.rearrange("p (t k) -> p t k", t=NT), AX, ALU.add))
            st.link(v.reciprocal(t8[3], t8[3]))
            v.wait_ge(s["counts"], 1)
            st.link(v.tensor_scalar(ntile, ps[:, 6, 0:E], 1.0 / P, 0.5 - 0.5 / P, ALU.mult, ALU.add))
            st.link(v.tensor_scalar(ntile, ntile, ROUND, -ROUND, ALU.add, ALU.add))
            st.link(v.tensor_tensor_scan(tend, ones[:, 0:E], ntile, 0.0, ALU.mult, ALU.add))
            st.link(v.tensor_tensor(base, tend, ntile, ALU.subtract))
            st.link(v.tensor_scalar(base, base, float(P), 1.0, ALU.mult, ALU.add))
            v.wait_ge(s["rank"], 1)
            st.link(v.tensor_tensor(key, bank(5).rearrange("p (t e) -> p t e", t=NT), base.unsqueeze(1).broadcast_to([P, NT, E]), ALU.add))
            st.link(v.tensor_tensor(key, key, mask, ALU.mult))
            for t in range(NT):
                st.add(v.max(out=slot8[:, K * t:K * t + K], in_=key[:, t, :]))
            st.wait()
            s0 = rest[:, 1, :]
            st.link(v.tensor_scalar(s0, slot8, -1.0, None, ALU.add))
            st.add(v.tensor_copy(slot, s0))
            st.link(v.tensor_scalar(icol, s0, 1.0 / P, -(0.5 - 0.5 / P), ALU.mult, ALU.add))
            st.link(v.tensor_scalar(icol, icol, ROUND, -ROUND, ALU.add, ALU.add))
            st.add(v.tensor_copy(tile16, icol))
            st.add(v.scalar_tensor_tensor(out=row16, in0=icol, scalar=-float(P), in1=s0, op0=ALU.mult, op1=ALU.add))
            st.wait()
            v.sem_inc(s["slots"], 1)
            st.link(v.tensor_scalar(rest[:, 2, :], tend, t8[0][:, 0:1], None, ALU.is_le))
            st.link(v.tensor_reduce(t8[4][:, 0:1], rest[:, 2, :], AX, ALU.add))
            v.tensor_scalar(t8[4][:, 0:1], t8[4][:, 0:1], float(E - 1), None, ALU.min).then_inc(s["te"], 1)
            v.wait_ge(s["ro_consts"], 1)
            for t in range(NT + 1):
                if t < NT:
                    if t == 0:
                        v.wait_ge(s["xln_stored"], 16)
                    if t >= 4:
                        v.wait_ge(s["onehots_read"], t - 3)
                    if t < DVE_ROWS:
                        st.add(v.tensor_tensor(hot_row[t], *spread_out(row16, t), ALU.is_equal))
                    eq = st.add(v.tensor_tensor(hot_tile[t % 4], *spread_out(tile16, t), ALU.is_equal))
                if t >= 1:
                    st.wait(eq_before if t < NT else eq)
                    v.tensor_scalar(hot_tile[(t - 1) % 4], hot_tile[(t - 1) % 4], t8[0][:, t - 1:t], None, ALU.mult).then_inc(s["onehots"], 1)
                eq_before = eq
            v.wait_ge(s["te_ps"], 1)
            v.tensor_copy(te_row, ps[0:1, 7, 0:P]).then_inc(s["te_row"], 1)
            v.wait_ge(s["idx_ps"], 1)
            v.tensor_copy(idx, ps[:, 6, 0:P]).then_inc(s["idx"], 1)

            def gate_up(i, n, turn):
                v.wait_ge(s["m_silu"], i + 1)
                if first_free(i, 2):
                    v.wait_ge(s["m_aT"], i - 1)
                v.tensor_tensor(act_buf[n % 2], ps[:, 2 + n % 2, I:I2], silu_buf[n % 2], ALU.mult).then_inc(s["m_act"], 1)

            def turn_act(i, n, turn):
                v.wait_ge(s["m_aT"], i + 1)
                if first_free(i, 2):
                    v.wait_ge(s["m_y_ps"], i - 1)
                v.tensor_copy(actT_buf[n % 2][0:I, :], ps[0:I, 4 + n % 2, 0:P]).then_inc(s["m_actT"], 1)

            def take_y(i, n, turn):
                v.wait_ge(s["m_y_ps"], i + 1)
                if first_free(i, STORES):
                    v.wait_ge(stored[n % STORES], turn * (16 * UNROLL // STORES) + 16 * (n // STORES))
                v.tensor_copy(y_buf[n % STORES], ps[:, 6 + n % 2, 0:H]).then_inc(s["m_y"], 1)

            skewed(v, [(1, gate_up), (0, turn_act), (-1, take_y)])

            st.link(v.tensor_tensor(wdense, probs, mask, ALU.mult))
            st.link(v.tensor_tensor(wdense, wdense, t8[3].unsqueeze(2).broadcast_to([P, NT, E]), ALU.mult))
            for n in range(NT * K):
                t = n // K
                st.add(v.scalar_tensor_tensor(out=unused[:, n, :], in0=key[:, t, :], scalar=slot8[:, n:n + 1], in1=wdense[:, t, :],
                                              op0=ALU.is_equal, op1=ALU.mult, accum_out=icol[:, n:n + 1]))
            st.wait()
            for t in range(NT):
                if t < NT - 1:
                    v.wait_ge(picked[t], 16 * K)
                for k in range(K):
                    n = t * K + k
                    if t == NT - 1:
                        v.wait_ge(picked_last[k], 16)
                    ins = v.scalar_tensor_tensor(out=xt[:, t, :], in0=picks[:, n, :], scalar=icol[:, n:n + 1], in1=xt[:, t, :], op0=ALU.mult, op1=ALU.add)
                    if k < K - 1:
                        st.link(ins)
                    else:
                        ins.then_inc(s["out_tile"], 1)

        @block.scalar
        def _(act):
            st = Steps(act, s["act_chain"])
            act.wait_ge(s["consts"], 1)
            st.add(act.copy(nmax, ident[:, 0:NT]))
            for i in range(2):
                act.wait_ge(s["ctxT_ps"], i + 1)
                act.copy(ctxT[:, 512 * i:512 * i + 512], bank(i)).then_inc(s["ctxT"], 1)
            act.wait_ge(s["stats"], 1)
            act.activation(rstd, rstd, ACT.Sqrt).then_inc(s["sq"], 1)
            for h in range(NH):
                act.wait_ge(s["xin_ps"], h + 1)
                act.copy(xin[:, h, :, TAPS - 1:TAPS - 1 + L], bank(4 + 2 * h, 2).rearrange("p (b l) -> p b l", b=B)).then_inc(s["xin"], 1)
            act.wait_ge(loaded["ffn"], 16 * 4)
            for i, raw in enumerate((w1_raw, w2_raw)):
                act.activation(big[:, 4096:6144], raw, ACT.Abs, accum_out=wsum[:, i:i + 1]).then_inc(s["wabs"], 1)
                act.wait_ge(s["wabs"], i + 1)
            act.wait_ge(loaded["vectors"], 16 * 10)

            def conv_silu(c):
                for h in range(NH):
                    act.wait_ge(s["conv"], NH * c + h + 1)
                    act.activation(u[:, h, 512 * c:512 * c + 512], conv[h][:, 512 * c:512 * c + 512], ACT.Silu).then_inc(s["u_ready"], 1)

            conv_silu(0)
            act.wait_ge(s["stats"], 2)
            for t in range(NT):
                b, h = t // LT, t % LT
                act.activation(z[:, h, b * L:(b + 1) * L], xt[:, t, :], ACT.Silu, bias=nbias[:, t:t + 1], scale=rstd[:, t:t + 1]).then_inc(s["z_ready"], 1)
            conv_silu(1)
            for c in range(2):
                for h in range(NH):
                    act.wait_ge(s["dpre_ps"], NH * c + h + 1)
                    act.activation(lb[c][:, 512 * h:512 * h + 512], bank(4 + 2 * h + c), ACT.Abs, bias=dtb[:, h:h + 1]).then_inc(s["xabs"], 1)
                act.wait_ge(s["xabs"], NH * c + NH)
                act.activation(lb[c], lb[c], ACT.Exp, scale=-1.0).then_inc(s["eneg"], 1)
                for h in range(NH):
                    act.activation(du[:, h, 512 * c:512 * c + 512], bank(4 + 2 * h + c), ACT.Relu, bias=dtb[:, h:h + 1]).then_inc(s["relu"], 1)
            act.wait_ge(s["bc_ps"], 1)
            act.copy(bcs, bank(0, 2)[0:96, :]).then_inc(s["bc_hi"], 1)
            st.link(act.activation(Aneg, Aneg, ACT.Exp))
            st.link(act.mul(Aneg, Aneg, -1.0))
            for c in range(2):
                act.wait_ge(s["eneg"], c + 1)
                act.activation(delta[:, :, 512 * c:512 * c + 512], lb[c].rearrange("p (h t) -> p h t", h=NH), ACT.Ln, bias=1.0).then_inc(s["lnp"], 1)
            for g in range(4):
                act.wait_ge(s["wqT_ps"], g + 1)
                dst = w1qT[:, g * FF:(g + 1) * FF] if g < 2 else w2qT[:, :].rearrange("p (k d) -> p k d", k=FK)[:, :, (g - 2) * P:(g - 1) * P]
                src = bank(2 + g % 2).bitcast(BF16)
                act.activation(dst, src if g < 2 else src.rearrange("p (k d) -> p k d", k=FK), ACT.Sign).then_inc(s["wqT"], 1)

            def decay(m):
                n, h = m // NH, m % NH
                if m >= 2:
                    act.wait_ge(s["scan"], m - 1)
                act.activation(lb[h].rearrange("p (b l) -> p b l", b=B)[:, :, 1:L],
                               delta[:, h, :].rearrange("p (b l) -> p b l", b=B)[:, :, 1:L],
                               ACT.Exp, scale=Aneg[:, h, n:n + 1]).then_inc(s["dA"], 1)

            def copy_b(n):
                act.wait_ge(s["bmat"], n + 1)
                if n >= 2:
                    act.wait_ge(s["dbu"], NH * (n - 1))
                act.copy(bsb[n % 2], bank(0, 2)).then_inc(s["b_copied"], 1)

            copy_b(0)
            act.wait_ge(s["delta_ready"], 2)
            act.wait_ge(s["sequence_starts"], 1)
            decay(0)
            for n in range(DS):
                decay(NH * n + 1)
                if n + 1 < DS:
                    copy_b(n + 1)
                    decay(NH * n + 2)
                if 1 <= n <= NT:
                    t = n - 1
                    act.wait_ge(s["attT_ps"], t + 1)
                    act.copy(attT[:, :, t // LT, (t % LT) * P:(t % LT + 1) * P], ps[:, 1, 0:2 * P].rearrange("p (k c) -> p k c", k=LT)).then_inc(s["attT"], 1)
                if n < NT:
                    act.wait_ge(s["att_max"], n + 1)
                    act.activation(ex[:, n % 2, :], ps[:, 0, 0:L], ACT.Exp, bias=nmax[:, n:n + 1], accum_out=asum[:, n:n + 1]).then_inc(s["att_exp"], 1)

            def variance_root(g):
                half = slice(g * (NT // 2), (g + 1) * (NT // 2))
                act.wait_ge(s["ffn_var"], g + 1)
                act.activation(rstd[:, half], rstd[:, half], ACT.Sqrt).then_inc(s["ffn_std"], 1)

            def rows_scaled(g):
                act.wait_ge(s["ffn_scale"], g + 1)
                for t in range(g * (NT // 2), (g + 1) * (NT // 2)):
                    act.activation(xn[:, t, :], xn[:, t, :], ACT.Identity, scale=t8[1][:, t:t + 1]).then_inc(s["xn"], 1)

            variance_root(0)
            rows_scaled(0)
            variance_root(1)
            for j in range(NT + 2):
                if j < NT:
                    act.wait_ge(s["h_ps"], j + 1)
                    if j >= 2:
                        act.wait_ge(s["h_ss"], j - 1)
                    act.activation(r_buf[j % 2], bank(2 * (j % 2), 2), ACT.Relu, scale=t8[4][:, j:j + 1]).then_inc(s["h_relu"], 1)
                    act.wait_ge(s["h_relu"], j + 1)
                    if j >= 2:
                        act.wait_ge(s["hg"], j - 1)
                    act.activation(h_buf[j % 2], r_buf[j % 2], ACT.Square).then_inc(s["h_sq"], 1)
                    if j == 0:
                        rows_scaled(1)
                if 1 <= j <= NT:
                    act.wait_ge(s["r2_var"], j)
                    act.activation(t8[5][:, j - 1:j], t8[5][:, j - 1:j], ACT.Sqrt).then_inc(s["r2_std"], 1)
                if j < NT:
                    act.wait_ge(s["h_sq"], j + 1)
                    act.activation(r_buf[j % 2], h_buf[j % 2], ACT.Square, accum_out=t8[5][:, j:j + 1]).then_inc(s["h_ss"], 1)
                if j >= 2:
                    t = j - 2
                    act.wait_ge(s["q2T_ps"], t + 1)
                    if t >= 2:
                        act.wait_ge(s["o_ps"], t - 1)
                    act.copy(q2T_buf[t % 2].rearrange("p k c -> p (k c)"), bank(4 + t % 2).bitcast(BF16)).then_inc(s["q2T"], 1)

            for name in ("at", "ro"):
                def root(g):
                    act.wait_ge(s[name + "_var"], g + 1)
                    half = rstd[:, g * (NT // 2):(g + 1) * (NT // 2)]
                    act.activation(half, half, ACT.Sqrt).then_inc(s[name + "_std"], 1)

                def turned(g):
                    act.wait_ge(s[name + "_lnT_ps"], g + 1)
                    act.copy(lnT[:, 2 * g:2 * g + 2, :, :].rearrange("p t k c -> p (t k c)"), bank(g)).then_inc(s[name + "_lnT"], 1)

                root(0)
                turned(0)
                turned(1)
                root(1)
                turned(2)
                turned(3)
            for g in range(2):
                act.wait_ge(s["logit_shift"], g + 1)
                half = probs[:, g * (NT // 2):(g + 1) * (NT // 2), :]
                act.activation(half, half, ACT.Exp).then_inc(s["logit_exp"], 1)

            for i in range(NT - DVE_ROWS):
                act.wait_ge(s["row_diffs"], i + 1)
                d = hot_row[DVE_ROWS + i % POOL_RING]
                st.link(act.activation(d, d, ACT.Abs))
                act.activation(d, d, ACT.Relu, scale=-1.0, bias=1.0).then_inc(s["row_onehots"], 1)

            st.add(act.activation(nmax, nmax, ACT.Silu))

            def take_gT(i, n, turn):
                act.wait_ge(s["m_T"], i + 1)
                if first_free(i, 2):
                    act.wait_ge(s["m_h"], i - 1)
                act.copy(gT_buf[n % 2], ps[:, n % 2, 0:H]).then_inc(s["m_gT"], 1)

            def silu(i, n, turn):
                act.wait_ge(s["m_h"], i + 1)
                if first_free(i, 2):
                    act.wait_ge(s["m_act"], i - 1)
                act.activation(silu_buf[n % 2], ps[:, 2 + n % 2, 0:I], ACT.Silu).then_inc(s["m_silu"], 1)

            skewed(act, [(2, take_gT), (1, silu)])

        @block.tensor
        def _(pe):
            pe.wait_ge(s["consts"], 1)
            pe.wait_ge(loaded["ctx"], 16)
            for t in range(NT):
                ins = pe.transpose(ps[:, t // 4, (t % 4) * P:(t % 4 + 1) * P], ctx_raw[:, t, :], ident[:])
                if t % 4 == 3:
                    ins.then_inc(s["ctxT_ps"], 1)
            pe.wait_ge(loaded["proj"], 16 * 5)
            for i, w in enumerate((inw_raw[:, 0, :], inw_raw[:, 1, :], wq_raw, wk_raw)):
                ins = pe.transpose(ps[:, 2, i * P:(i + 1) * P], w, ident[:])
            ins.then_inc(s["wT_ps"], 1)
            nx = DR + 2 * DS
            for k in range(NH):
                pe.transpose(ps[:, 3, 64 * k:64 * k + nx], xp_raw[:, k * P:(k + 1) * P], ident[0:nx, 0:nx])
                ins = pe.transpose(ps[0:DR, 3, (k + 1) * P:(k + 2) * P], dt_raw[:, k, :], ident[:])
            ins.then_inc(s["wT_ps"], 1)
            pe.wait_ge(s["ctxT"], 2)
            pe.wait_ge(s["wT"], 1)
            for h in range(NH):
                for c in range(2):
                    ins = pe.matmul(bank(4 + 2 * h + c), wT[:, h * P:(h + 1) * P], ctxT[:, c * 512:(c + 1) * 512], start=True, stop=True)
                ins.then_inc(s["xin_ps"], 1)
            pe.wait_ge(s["wT"], 2)
            for k in range(NH):
                ins = pe.matmul(ps[:, 2, k * DI:(k + 1) * DI], xp_raw[0:DR, k * P:(k + 1) * P], dtT, start=True, stop=True)
            ins.then_inc(s["dtxT_ps"], 1)
            for i in range(2):
                if i == 1:
                    pe.wait_ge(s["dtxT"], 1)
                for c in range(2):
                    ins = pe.matmul(bank(2 * i + c), wT[:, (2 + i) * P:(3 + i) * P], ctxT[:, c * 512:(c + 1) * 512], start=True, stop=True)
                ins.then_inc(s["qk_ps"], 1)
            pe.wait_ge(s["wabs"], 2)
            pe.wait_ge(s["xin"], NH)
            pe.matmul(ps[:, 4, 0:2], ones, wsum, start=True, stop=True).then_inc(s["wtot"], 1)
            pe.wait_ge(s["wmean_ready"], 1)
            pe.wait_ge(s["dtxT"], 1)
            pe.wait_ge(s["xin"], NH)
            for c in range(2):
                pe.wait_ge(s["u_ready"], NH * (c + 1))
                for h in range(NH):
                    for k in range(NH):
                        ins = pe.matmul(bank(4 + 2 * h + c), dtxT[:, k, h * P:(h + 1) * P], u[:, k, c * 512:(c + 1) * 512], start=k == 0, stop=k == NH - 1)
                    ins.then_inc(s["dpre_ps"], 1)
            pe.wait_ge(s["qk"], 1)
            for c in range(2):
                for k in range(NH):
                    ins = pe.matmul(ps[0:96, c, :], xpT[:, k, :], u[:, k, c * 512:(c + 1) * 512], start=k == 0, stop=k == NH - 1)
            ins.then_inc(s["bc_ps"], 1)
            pe.wait_ge(s["qk"], 2)
            for g in range(4):
                pe.wait_ge(s["wquant"], g // 2 + 1)
                if g >= 2:
                    pe.wait_ge(s["wqT"], g - 1)
                dst = bank(2 + g % 2).bitcast(BF16)
                for j in range(8):
                    if g < 2:
                        src = w1q[:, j * DM + g * P:j * DM + (g + 1) * P]
                    else:
                        src = w2q[:, (g - 2) * FF + j * P:(g - 2) * FF + (j + 1) * P]
                    ins = pe.transpose(dst[:, j * P:(j + 1) * P], src, identb[:])
                ins.then_inc(s["wqT_ps"], 1)
            pe.wait_ge(s["bc"], 1)

            def spread(at, row, done):
                for c in range(2):
                    ins = pe.matmul(bank(at + c), sel[:, row:row + 1].broadcast_to([96, P]), bcs[:, c * 512:(c + 1) * 512], start=True, stop=True)
                ins.then_inc(done, 1)

            def spread_b(n):
                if n >= 1:
                    pe.wait_ge(s["b_copied"], n)
                spread(0, n, s["bmat"])

            spread_b(0)
            pe.wait_ge(s["wqT"], 4)
            spread(2, DS, s["cmat"])
            spread_b(1)
            pe.wait_ge(s["relu"], 2 * NH)
            for m in range(STEPS):
                n, h = m // NH, m % NH
                pe.wait_ge(s["hc"], m + 1)
                if h == 1 and n + 1 < DS:
                    spread(2, DS + n + 1, s["cmat"])
                if h == 1 and NT <= n < DS - 2:
                    if n == NT:
                        pe.wait_ge(s["attT"], NT)
                    spread_b(n + 2)
                for c in range(2):
                    ins = pe.matmul(bank(4 + 2 * h + c), ident[:], lb[6 + h][:, c * 512:(c + 1) * 512], start=n == 0, stop=n == DS - 1)
                ins.then_inc(s["ysum"], 1)
                if h == 0 and n < NT:
                    pe.wait_ge(s["b_copied"], n + 2)
                    pe.matmul(ps[:, 0, 0:L], qT[:, n * P:(n + 1) * P], kT[:, (n // LT) * L:(n // LT + 1) * L], start=True, stop=True
                              ).then_inc(s["energy"], 1)
                if h == 0 and 1 <= n <= NT:
                    t = n - 1
                    pe.wait_ge(s["att_norm"], t + 1)
                    pe.wait_ge(s["b_copied"], n + 2)
                    for k in range(LT):
                        ins = pe.transpose(ps[:, 1, k * P:(k + 1) * P], ex[:, t % 2, k * P:(k + 1) * P], ident[:])
                    ins.then_inc(s["attT_ps"], 1)
                if h == 1 and n < NT:
                    pe.wait_ge(s["att_exp"], n + 1)
                    if n >= 1:
                        pe.wait_ge(s["attT"], n)
                    spread_b(n + 2)
            for t in range(NT):
                pe.wait_ge(s["y_ready"], 2 + t // (NT // 2))
                for h in range(NH):
                    ins = pe.transpose(ps[:, t // 2, ((t % 2) * NH + h) * P:((t % 2) * NH + h + 1) * P], du[:, h, t * P:(t + 1) * P], ident[:])
                if t % 2 == 1:
                    ins.then_inc(s["yT_ps"], 1)

            def ffn_turn_in(g):
                pe.wait_ge(s["q1"], g + 1)
                for t in range(NT // 2):
                    for k in range(KH):
                        ins = pe.transpose(bank(6 + g).bitcast(BF16)[:, (t * KH + k) * P:(t * KH + k + 1) * P], q1[:, g * (NT // 2) + t, k * P:(k + 1) * P], identb[:])
                ins.then_inc(s["q1T_ps"], 1)

            def ffn_up(t):
                pe.wait_ge(s["q1T"], t // 4 + 1)
                pe.wait_ge(s["x1"], NT // 2)
                if t >= 2:
                    pe.wait_ge(s["h_relu"], t - 1)
                for c in range(2):
                    for k in range(KH):
                        ins = pe.matmul(bank(2 * (t % 2) + c), q1T[:, k, t * P:(t + 1) * P], w1T[:, k, c * 512:(c + 1) * 512], start=k == 0, stop=k == KH - 1)
                ins.then_inc(s["h_ps"], 1)

            def ffn_turn(t):
                pe.wait_ge(s["q2"], t + 1)
                if t >= 2:
                    pe.wait_ge(s["q2T"], t - 1)
                for k in range(FK):
                    ins = pe.transpose(bank(4 + t % 2).bitcast(BF16)[:, k * P:(k + 1) * P], q2_buf[t % 2][:, k * P:(k + 1) * P], identb[:])
                ins.then_inc(s["q2T_ps"], 1)

            def ffn_down(t):
                pe.wait_ge(s["q2T"], t + 1)
                pe.wait_ge(s["q1T"], 2)
                if t >= 2:
                    pe.wait_ge(s["x2"], t - 1)
                for k in range(FK):
                    ins = pe.matmul(ps[:, 6 + t % 2, 0:DM], q2T_buf[t % 2][:, k, :], w2T[:, k, :], start=k == 0, stop=k == FK - 1)
                ins.then_inc(s["o_ps"], 1)

            ffn_turn_in(0)
            for j in range(NT + 3):
                if j == 2:
                    ffn_turn_in(1)
                for off, part_ in ((0, ffn_up), (-2, ffn_turn), (-3, ffn_down)):
                    if 0 <= j + off < NT:
                        part_(j + off)

            def turn_ln(name, tiles):
                for t in tiles:
                    pe.wait_ge(s[name + "_ln"], t + 1)
                    for k in range(KH):
                        ins = pe.transpose(ps[:, t // 2, ((t % 2) * KH + k) * P:((t % 2) * KH + k + 1) * P], ln[:, t, k * P:(k + 1) * P], ident[:])
                    if t % 2 == 1:
                        ins.then_inc(s[name + "_lnT_ps"], 1)

            def attend(tiles):
                for t in tiles:
                    if t == 0:
                        pe.wait_ge(s["q2T"], NT)
                    if t == 2:
                        pe.wait_ge(s["x2"], NT)
                    pe.wait_ge(s["at_lnT"], t // 2 + 1)
                    if t >= 4:
                        pe.wait_ge(s["x3"], t - 3)
                    for k in range(LT):
                        ins = pe.matmul(ps[:, 4 + t % 4, 0:L], lnT[:, t, k, :], attT[:, k, t // LT, :], start=k == 0, stop=k == LT - 1)
                    ins.then_inc(s["at_ps"], 1)

            turn_ln("at", range(4))
            attend(range(2))
            turn_ln("at", range(4, 6))
            attend(range(2, 4))
            turn_ln("at", range(6, 8))
            attend(range(4, 8))

            def gate_logits(tiles):
                for t in tiles:
                    pe.wait_ge(s["ro_lnT"], t // 2 + 1)
                    for k in range(KH):
                        at = (t % (NT // 2)) * E
                        ins = pe.matmul(ps[:, 4 + 3 * (t // (NT // 2)), at:at + E], lnT[:, t, k, :], wgate[:, k, :], start=k == 0, stop=k == KH - 1)
                    if t % (NT // 2) == NT // 2 - 1:
                        ins.then_inc(s["logits"], 1)

            turn_ln("ro", range(4))
            pe.wait_ge(s["x3"], NT)
            gate_logits(range(4))
            turn_ln("ro", range(4, 8))
            gate_logits(range(4, 8))
            def ranks(tiles):
                for t in tiles:
                    for j in range(t):
                        pe.matmul(ps[:, 5, t * E:(t + 1) * E], onesb, mask[:, j, :], start=j == 0, stop=False)
                    ins = pe.matmul(ps[:, 5, t * E:(t + 1) * E], before, mask[:, t, :], start=t == 0, stop=True)
                return ins

            pe.wait_ge(s["mask"], 1)
            pe.wait_ge(s["ro_consts"], 1)
            ranks(range(4))
            pe.wait_ge(s["mask"], 2)
            for t in range(NT):
                ins = pe.matmul(ps[:, 6, 0:E], onesb, mask[:, t, :], start=t == 0, stop=t == NT - 1)
            ins.then_inc(s["counts"], 1)
            ranks(range(4, 8)).then_inc(s["rank"], 1)
            pe.wait_ge(s["te"], 1)
            pe.transpose(ps[0:1, 7, 0:P], t8[4][:, 0:1], ident[:]).then_inc(s["te_ps"], 1)
            for t in range(NT):
                pe.wait_ge(s["onehots"], t + 1)
                if t >= DVE_ROWS:
                    pe.wait_ge(s["row_onehots"], t - DVE_ROWS + 1)
                rows = hot_row[t if t < DVE_ROWS else DVE_ROWS + (t - DVE_ROWS) % POOL_RING]
                for k in range(K):
                    ins = pe.matmul(ps[:, 6, 0:P], rows[:, k, :], hot_tile[t % 4][:, k, :], start=t == k == 0, stop=t == NT - 1 and k == K - 1)
                ins.then_inc(s["onehots_read"], 1)
            pe.wait_ge(s["onehots_read"], NT)
            pe.sem_inc(s["idx_ps"], 1)

            expert_regs = [pe.alloc_register(f"expert{r}") for r in range(4)]

            def load_expert(i, n):
                pe.load(expert_regs[n % 4], te_row[0:1, bass.ds(i, 1)])

            def expert(n):
                return pe.snap(expert_regs[n % 4], min_val=0, max_val=E - 1)

            def turn_g(i, n, turn):
                pe.wait_ge(gathered[n % GATHERS], turn * (16 * UNROLL // GATHERS) + 16 * (n // GATHERS) + 16)
                if first_free(i, 2):
                    pe.wait_ge(s["m_gT"], i - 1)
                for k in range(KH):
                    ins = pe.transpose(ps[:, n % 2, k * P:(k + 1) * P], g_buf[n % GATHERS][:, k * P:(k + 1) * P], ident[:])
                ins.then_inc(s["m_T"], 1)

            down_at = {}

            def up(i, n, turn):
                e = expert(n)
                pe.wait_ge(s["m_gT"], i + 1)
                if first_free(i, 2):
                    pe.wait_ge(s["m_act"], i - 1)
                for k in range(KH):
                    ins = pe.matmul(ps[:, 2 + n % 2, 0:I2], gT_buf[n % 2][:, k * P:(k + 1) * P],
                                    w13[:, bass.ds(e * (KH * I2) + k * I2, I2)], start=k == 0, stop=k == KH - 1)
                ins.then_inc(s["m_h"], 1)
                if not isinstance(i, int) or i >= 2:
                    down_at[(n - 2) % UNROLL] = pe.snap(expert(n - 2) * H, min_val=0, max_val=(E - 1) * H)
                if not isinstance(i, int) or i + 1 < MT:
                    load_expert(i + 1, n + 1)

            def turn_act(i, n, turn):
                pe.wait_ge(s["m_act"], i + 1)
                if first_free(i, 2):
                    pe.wait_ge(s["m_actT"], i - 1)
                pe.transpose(ps[0:I, 4 + n % 2, 0:P], act_buf[n % 2], ident[:]).then_inc(s["m_aT"], 1)

            def down(i, n, turn):
                at = down_at.pop(n) if n in down_at else expert(n) * H
                pe.wait_ge(s["m_actT"], i + 1)
                if first_free(i, 2):
                    pe.wait_ge(s["m_y"], i - 1)
                pe.matmul(ps[:, 6 + n % 2, 0:H], actT_buf[n % 2][0:I, :], big[0:I, bass.ds(at, H)], start=True, stop=True).then_inc(s["m_y_ps"], 1)

            pe.wait_ge(s["te_row"], 1)
            pe.wait_ge(s["idx"], 1)
            pe.wait_ge(loaded["w13"], 16 * (E // EC))
            pe.wait_ge(loaded["w2e"], 16 * 4)
            load_expert(0, 0)
            skewed(pe, [(2, turn_g), (1, up), (0, turn_act), (-1, down)])


_INS = ['x', 'ctx_1024', 'L0_xattn_in_proj_w', 'L0_xattn_conv_w', 'L0_xattn_conv_b', 'L0_xattn_x_proj_w', 'L0_xattn_dt_proj_w',
        'L0_xattn_dt_proj_b', 'L0_xattn_A_log', 'L0_xattn_D', 'L0_ffn_w1', 'L0_ffn_g1', 'L0_ffn_w2', 'L0_ffn_g2',
        'L1_xattn_Wq', 'L1_xattn_bq', 'L1_xattn_Wk', 'L1_xattn_bk', 'L1_ffn_w_gate', 'L1_ffn_w13', 'L1_ffn_w2']


def kernel(**inputs):
    import numpy as _np
    import concourse.bacc as _bacc
    from concourse import mybir as _mybir
    from concourse.bass_utils import run_bass_kernel_spmd as _run

    nc = _bacc.Bacc("TRN2", target_bir_lowering=False, num_devices=1)
    arrays, args = {}, {}
    for name in _INS:
        v = _np.ascontiguousarray(inputs[name])
        arrays[f"in_{name}_dram"] = v
        args[name] = nc.dram_tensor(f"in_{name}_dram", v.shape, _mybir.dt.from_np(v.dtype), kind="ExternalInput").ap()
    out = nc.dram_tensor("out_0_dram", args["x"].shape, F32, kind="ExternalOutput").ap()
    xln_dram = nc.dram_tensor("xln_dram", (1024, 256), F32, kind="Internal").ap()
    y_dram = nc.dram_tensor("y_dram", (128 * 128, 256), F32, kind="Internal").ap()
    mamba_ffn_attention_moe(nc, args, out, xln_dram, y_dram)
    r = _run(nc, [arrays], core_ids=[0])
    return r.results[0]["out_0_dram"]
```
